# Optimizing a Trainium2 kernel written in Bass

```python
import numpy as np
import jax
import jax.numpy as jnp

def _softmax(x, axis=-1):
    return jax.nn.softmax(x, axis=axis)

def _gelu(x):
    return jax.nn.gelu(x, approximate=True)

def _silu(x):
    return jax.nn.silu(x)

def _sigmoid(x):
    return jax.nn.sigmoid(x)

def _layernorm(x, axis=-1, eps=1e-05):
    m = jnp.mean(x, axis=axis, keepdims=True)
    v = jnp.var(x, axis=axis, keepdims=True)
    return (x - m) / jnp.sqrt(v + eps)

def _scatter_add(tgt, idx, src, axis=0):
    return tgt.at[idx].add(src)

def _segment_sum(src, seg, n):
    return jax.ops.segment_sum(src, seg, n)
kernel_name = 'mk_seq_postln_d1_jaxref_r8_52e850'

def setup_inputs(seed: int=0):
    np.random.seed(seed)
    _w = jnp.asarray

    def _L0_attn_setup():
        import jax, jax.numpy as jnp
        import numpy as np
        D = 128
        H = 16
        KVH = 4
        HD = D // H
        LAT = 32
        WIN = 32
        B, S = (1, 256)
        BASE_G, BASE_L = (1000000.0, 10000.0)
        EPS = 1e-06

        def rmsnorm(x, w):
            return x * jax.lax.rsqrt(jnp.mean(x * x, axis=-1, keepdims=True) + EPS) * w

        def qk_norm(x):
            return x * jax.lax.rsqrt(jnp.mean(x * x, axis=-1, keepdims=True) + EPS)

        def rope(x, base):
            s, hd = (x.shape[-2], x.shape[-1])
            inv_freq = 1.0 / base ** (jnp.arange(0, hd, 2, dtype=jnp.float32) / hd)
            freqs = jnp.arange(s, dtype=jnp.float32)[:, None] * inv_freq[None, :]
            cos, sin = (jnp.cos(freqs), jnp.sin(freqs))
            xe, xo = (x[..., ::2], x[..., 1::2])
            out = jnp.stack([xe * cos - xo * sin, xe * sin + xo * cos], axis=-1)
            return out.reshape(x.shape)

        def split_heads(x, n_heads):
            b, s, _ = x.shape
            return x.reshape(b, s, n_heads, HD).transpose(0, 2, 1, 3)

        def repeat_kv(x):
            return jnp.repeat(x, H // KVH, axis=1)

        def sdpa(q, k, v, mask):
            scores = jnp.einsum('bhqd,bhkd->bhqk', q, k) / np.sqrt(HD).astype(np.float32)
            scores = jnp.where(mask, scores, jnp.float32(-1e+30))
            probs = jax.nn.softmax(scores, axis=-1)
            return jnp.einsum('bhqk,bhkd->bhqd', probs, v)

        def merge_heads(x):
            b, h, s, hd = x.shape
            return x.transpose(0, 2, 1, 3).reshape(b, s, h * hd)

        def global_latent_attn(x, wq, w_kv_down, w_k_up, w_v_up, wo):
            q = split_heads(x @ wq, H)
            latent = x @ w_kv_down
            k = split_heads(latent @ w_k_up, KVH)
            v = split_heads(latent @ w_v_up, KVH)
            q, k = (rope(q, BASE_G), rope(k, BASE_G))
            q, k = (qk_norm(q), qk_norm(k))
            k, v = (repeat_kv(k), repeat_kv(v))
            i = jnp.arange(x.shape[1])
            causal = i[:, None] >= i[None, :]
            return merge_heads(sdpa(q, k, v, causal)) @ wo

        def local_gqa_attn(x, wq, wk, wv, wo):
            q = split_heads(x @ wq, H)
            k = split_heads(x @ wk, KVH)
            v = split_heads(x @ wv, KVH)
            q, k = (rope(q, BASE_L), rope(k, BASE_L))
            q, k = (qk_norm(q), qk_norm(k))
            k, v = (repeat_kv(k), repeat_kv(v))
            i = jnp.arange(x.shape[1])
            diff = i[:, None] - i[None, :]
            mask = (diff >= 0) & (diff < WIN)
            return merge_heads(sdpa(q, k, v, mask)) @ wo
        key = jax.random.key(seed)
        ks = jax.random.split(key, 12)
        std = 0.02
        return {'hidden': jax.random.normal(ks[0], (B, S, D), dtype=jnp.float32), 'norm1_w': jnp.ones((D,), jnp.float32), 'norm2_w': jnp.ones((D,), jnp.float32), 'g_wq': jax.random.normal(ks[1], (D, H * HD), jnp.float32) * std, 'g_kv_down': jax.random.normal(ks[2], (D, LAT), jnp.float32) * std, 'g_k_up': jax.random.normal(ks[3], (LAT, KVH * HD), jnp.float32) * std, 'g_v_up': jax.random.normal(ks[4], (LAT, KVH * HD), jnp.float32) * std, 'g_wo': jax.random.normal(ks[5], (D, D), jnp.float32) * std, 'l_wq': jax.random.normal(ks[6], (D, H * HD), jnp.float32) * std, 'l_wk': jax.random.normal(ks[7], (D, KVH * HD), jnp.float32) * std, 'l_wv': jax.random.normal(ks[8], (D, KVH * HD), jnp.float32) * std, 'l_wo': jax.random.normal(ks[9], (D, D), jnp.float32) * std}
    _L0_attn_in = _L0_attn_setup()

    def _L0_ffn_setup():
        import jax, jax.numpy as jnp
        import numpy as np
        EPS = 1e-05

        def _quantize(W):
            gamma = jnp.mean(jnp.abs(W))
            return jnp.clip(jnp.round(W / (gamma + EPS)), -1.0, 1.0)
        key = jax.random.key(seed)
        k_x, k_w1, k_b1, k_w2, k_b2 = jax.random.split(key, 5)
        n_embd = 128
        d_ff = 4 * n_embd
        B, S = (4, 512)
        bound1 = 1.0 / np.sqrt(n_embd)
        bound2 = 1.0 / np.sqrt(d_ff)
        x = jax.random.normal(k_x, (B, S, n_embd), dtype=jnp.float32)
        W1 = jax.random.uniform(k_w1, (d_ff, n_embd), jnp.float32, -bound1, bound1)
        b1 = jax.random.uniform(k_b1, (d_ff,), jnp.float32, -bound1, bound1)
        W2 = jax.random.uniform(k_w2, (n_embd, d_ff), jnp.float32, -bound2, bound2)
        b2 = jax.random.uniform(k_b2, (n_embd,), jnp.float32, -bound2, bound2)
        return {'x': x, 'W1': W1, 'b1': b1, 'W2': W2, 'b2': b2}
    _L0_ffn_in = _L0_ffn_setup()
    _d = {'L0_attn_hidden': _L0_attn_in['hidden'], 'L0_attn_norm1_w': _L0_attn_in['norm1_w'], 'L0_attn_norm2_w': _L0_attn_in['norm2_w'], 'L0_attn_g_wq': _L0_attn_in['g_wq'], 'L0_attn_g_kv_down': _L0_attn_in['g_kv_down'], 'L0_attn_g_k_up': _L0_attn_in['g_k_up'], 'L0_attn_g_v_up': _L0_attn_in['g_v_up'], 'L0_attn_g_wo': _L0_attn_in['g_wo'], 'L0_attn_l_wq': _L0_attn_in['l_wq'], 'L0_attn_l_wk': _L0_attn_in['l_wk'], 'L0_attn_l_wv': _L0_attn_in['l_wv'], 'L0_attn_l_wo': _L0_attn_in['l_wo'], 'L0_ffn_W1': _L0_ffn_in['W1'], 'L0_ffn_b1': _L0_ffn_in['b1'], 'L0_ffn_W2': _L0_ffn_in['W2'], 'L0_ffn_b2': _L0_ffn_in['b2']}
    _x0 = _d['L0_attn_hidden']
    _d['L0_attn_hidden'] = jax.random.normal(jax.random.fold_in(jax.random.key(seed), 1), (2, 1024, 128), dtype=_x0.dtype)
    del _x0
    return _d

def reference(L0_attn_hidden, L0_attn_norm1_w, L0_attn_norm2_w, L0_attn_g_wq, L0_attn_g_kv_down, L0_attn_g_k_up, L0_attn_g_v_up, L0_attn_g_wo, L0_attn_l_wq, L0_attn_l_wk, L0_attn_l_wv, L0_attn_l_wo, L0_ffn_W1, L0_ffn_b1, L0_ffn_W2, L0_ffn_b2):

    def _L0_attn_ref(hidden, norm1_w, norm2_w, g_wq, g_kv_down, g_k_up, g_v_up, g_wo, l_wq, l_wk, l_wv, l_wo):
        import jax, jax.numpy as jnp
        import numpy as np
        D = 128
        H = 16
        KVH = 4
        HD = D // H
        LAT = 32
        WIN = 32
        B, S = (1, 256)
        BASE_G, BASE_L = (1000000.0, 10000.0)
        EPS = 1e-06

        def rmsnorm(x, w):
            return x * jax.lax.rsqrt(jnp.mean(x * x, axis=-1, keepdims=True) + EPS) * w

        def qk_norm(x):
            return x * jax.lax.rsqrt(jnp.mean(x * x, axis=-1, keepdims=True) + EPS)

        def rope(x, base):
            s, hd = (x.shape[-2], x.shape[-1])
            inv_freq = 1.0 / base ** (jnp.arange(0, hd, 2, dtype=jnp.float32) / hd)
            freqs = jnp.arange(s, dtype=jnp.float32)[:, None] * inv_freq[None, :]
            cos, sin = (jnp.cos(freqs), jnp.sin(freqs))
            xe, xo = (x[..., ::2], x[..., 1::2])
            out = jnp.stack([xe * cos - xo * sin, xe * sin + xo * cos], axis=-1)
            return out.reshape(x.shape)

        def split_heads(x, n_heads):
            b, s, _ = x.shape
            return x.reshape(b, s, n_heads, HD).transpose(0, 2, 1, 3)

        def repeat_kv(x):
            return jnp.repeat(x, H // KVH, axis=1)

        def sdpa(q, k, v, mask):
            scores = jnp.einsum('bhqd,bhkd->bhqk', q, k) / np.sqrt(HD).astype(np.float32)
            scores = jnp.where(mask, scores, jnp.float32(-1e+30))
            probs = jax.nn.softmax(scores, axis=-1)
            return jnp.einsum('bhqk,bhkd->bhqd', probs, v)

        def merge_heads(x):
            b, h, s, hd = x.shape
            return x.transpose(0, 2, 1, 3).reshape(b, s, h * hd)

        def global_latent_attn(x, wq, w_kv_down, w_k_up, w_v_up, wo):
            q = split_heads(x @ wq, H)
            latent = x @ w_kv_down
            k = split_heads(latent @ w_k_up, KVH)
            v = split_heads(latent @ w_v_up, KVH)
            q, k = (rope(q, BASE_G), rope(k, BASE_G))
            q, k = (qk_norm(q), qk_norm(k))
            k, v = (repeat_kv(k), repeat_kv(v))
            i = jnp.arange(x.shape[1])
            causal = i[:, None] >= i[None, :]
            return merge_heads(sdpa(q, k, v, causal)) @ wo

        def local_gqa_attn(x, wq, wk, wv, wo):
            q = split_heads(x @ wq, H)
            k = split_heads(x @ wk, KVH)
            v = split_heads(x @ wv, KVH)
            q, k = (rope(q, BASE_L), rope(k, BASE_L))
            q, k = (qk_norm(q), qk_norm(k))
            k, v = (repeat_kv(k), repeat_kv(v))
            i = jnp.arange(x.shape[1])
            diff = i[:, None] - i[None, :]
            mask = (diff >= 0) & (diff < WIN)
            return merge_heads(sdpa(q, k, v, mask)) @ wo
        x = hidden
        x = x + global_latent_attn(rmsnorm(x, norm1_w), g_wq, g_kv_down, g_k_up, g_v_up, g_wo)
        x = x + local_gqa_attn(rmsnorm(x, norm2_w), l_wq, l_wk, l_wv, l_wo)
        return x

    def _L0_ffn_ref(x, W1, b1, W2, b2):
        import jax, jax.numpy as jnp
        import numpy as np
        EPS = 1e-05

        def _quantize(W):
            gamma = jnp.mean(jnp.abs(W))
            return jnp.clip(jnp.round(W / (gamma + EPS)), -1.0, 1.0)
        Wq1 = _quantize(W1)
        Wq2 = _quantize(W2)
        h = jax.nn.relu(jnp.einsum('bsd,fd->bsf', x, Wq1) + b1)
        out = jnp.einsum('bsf,df->bsd', h, Wq2) + b2
        return out
    x = L0_attn_hidden
    x = _layernorm(x + _L0_attn_ref(x, L0_attn_norm1_w, L0_attn_norm2_w, L0_attn_g_wq, L0_attn_g_kv_down, L0_attn_g_k_up, L0_attn_g_v_up, L0_attn_g_wo, L0_attn_l_wq, L0_attn_l_wk, L0_attn_l_wv, L0_attn_l_wo), axis=-1)
    x = _layernorm(x + _L0_ffn_ref(x, L0_ffn_W1, L0_ffn_b1, L0_ffn_W2, L0_ffn_b2), axis=-1)
    return x

_drawn_inputs = setup_inputs


def setup_inputs(seed=0):
    import zlib

    import numpy as np

    out = dict(_drawn_inputs(seed))
    spreads = {'L0_attn_norm1_w': (1.0, 0.6), 'L0_attn_norm2_w': (1.0, 0.6)}
    factors = {'L0_attn_g_wq': 8.0,
     'L0_attn_g_kv_down': 8.0,
     'L0_attn_g_k_up': 8.0,
     'L0_attn_g_v_up': 8.0,
     'L0_attn_g_wo': 8.0,
     'L0_attn_l_wq': 8.0,
     'L0_attn_l_wk': 8.0,
     'L0_attn_l_wv': 8.0,
     'L0_attn_l_wo': 8.0,
     'L0_ffn_b1': 8.0,
     'L0_ffn_b2': 200.0}
    for name, (base, spread) in spreads.items():
        noise = np.random.default_rng([zlib.crc32(name.encode()), seed]).standard_normal(out[name].shape)
        drawn = base * np.exp(spread * noise) if base else spread * noise
        out[name] = jnp.asarray(drawn.astype(out[name].dtype))
    for name, factor in factors.items():
        out[name] = (out[name] * factor).astype(out[name].dtype)
    return out
```

```python
from contextlib import ExitStack

import numpy as np

import concourse.bass as bass
from concourse import mybir

BATCH, SEQ, D = 2, 1024, 128
HEADS, KV_HEADS, HD, LATENT, WIN = 16, 4, 8, 32, 32
GROUP = HEADS // KV_HEADS
FF = 4 * D
P = 128
TILES = BATCH * SEQ // P
KT = SEQ // P
CT = 4
CHUNK = CT * P
CHUNKS = TILES // CT
UNITS = BATCH * KV_HEADS
QW, KVW = HEADS * HD, KV_HEADS * HD
QKW = QW + KVW
QKH = HEADS + KV_HEADS
PARTS = 3
ROWS3 = PARTS * HD
STACK = PARTS * ROWS3
BANK = 512
SCALE = float(1.0 / np.sqrt(np.float32(HD)))
BASES = (1000000.0, 10000.0)
EPS_RMS, EPS_LN, EPS_Q = 1e-6, 1e-5, 1e-5
MASKED = -1e30


def score_fills():
    fills = []
    for qc in range(SEQ // CHUNK):
        lo = qc * CHUNK
        first = lo // P
        for kt in range(first + 1):
            fills += [[(h, kt, lo, CHUNK)] for h in range(GROUP)]
        fills += [[(h, first + 1, lo + P, CHUNK - P), (h, first + 3, lo + 3 * P, P)] for h in range(GROUP)]
        fills += [[(h, first + 2, lo + 2 * P, 2 * P), (h + 1, first + 2, lo + 2 * P, 2 * P)]
                  for h in range(0, GROUP, 2)]
    return fills


FILLS = score_fills()
PER_STEP = 3
STEPS = len(FILLS) // PER_STEP
FILLS_QC0 = 10
assert len(FILLS) == STEPS * PER_STEP


def diagonal_runs(step):
    runs = []
    for n in range(PER_STEP):
        at, cols = 0, []
        for _, kt, q0, w in FILLS[PER_STEP * step + n]:
            if kt * P == q0:
                cols.append(at)
            at += w
        if cols and runs and runs[-1][2] == cols and runs[-1][0] + runs[-1][1] == n:
            runs[-1][1] += 1
        elif cols:
            runs.append([n, 1, cols])
    return runs


MASKED_STEPS = [s for s in range(STEPS) if diagonal_runs(s)]
LOCAL_STEPS = 2


def build(nc, hidden, norm1_w, norm2_w, g_wq, g_kv_down, g_k_up, g_v_up, g_wo,
          l_wq, l_wk, l_wv, l_wo, w1, b1, w2, b2, rope_tab, out):
    F32, BF16 = mybir.dt.float32, mybir.dt.bfloat16
    ACT, ALU, AX = mybir.ActivationFunctionType, mybir.AluOpType, mybir.AxisListType
    ctx = ExitStack()
    with ctx:
        def sb(name, shape, dt=F32):
            return ctx.enter_context(nc.sbuf_tensor(name, shape, dt))

        def sem(name):
            return ctx.enter_context(nc.semaphore(name))

        x0 = sb("x0", [P, TILES, D])
        x1 = sb("x1", [P, TILES, D])
        heads_out = sb("heads_out", [P, TILES, D])
        v_all = sb("v_all", [P, TILES, KVW])
        v_prev = sb("v_prev", [P, TILES, KVW])
        q_parts = sb("q_parts", [GROUP * ROWS3, UNITS, SEQ], BF16)
        k_stacks = sb("k_stacks", [STACK, UNITS, SEQ], BF16)
        ident = sb("ident", [P, P])
        ident_bf = sb("ident_bf", [P, P], BF16)
        ones = sb("ones", [P, P])
        band = sb("band", [P, 2, 2, GROUP * WIN], BF16)
        rope = sb("rope", [P, KT, 2, 2 * HD])
        nw = [sb("nw_global", [P, 1]), sb("nw_local", [P, 1])]
        wqkv_g = sb("wq_g", [P, QW])
        wdown = sb("wdown", [P, LATENT])
        wup = sb("wup", [LATENT, 2 * KVW])
        wqkv_l = sb("wqkv_l", [P, QKW + KVW])
        wo = [sb("wo_g", [P, D]), sb("wo_l", [P, D])]
        w1n, w2n = sb("w1n", [P, CT, D]), sb("w2n", [P, FF])
        w1q, w2q = sb("w1q", [P, FF]), sb("w2q", [P, CT, D])
        b1c = sb("b1c", [P, FF // P])
        b2b = sb("b2b", [P, D])
        sq = sb("sq", [P, CT, QKW])
        ssum = sb("ssum", [P, CT])
        sroot = sb("sroot", [P, CT])
        sinv = sb("sinv", [P, CT])
        xs = [sb(f"xs{i}", [P, CT, D]) for i in range(2)]
        xn_t = [sb(f"xn_t{i}", [P, CHUNK]) for i in range(2)]
        lat_t = [sb(f"lat_t{i}", [LATENT, CHUNK]) for i in range(2)]
        rot = sb("rot", [P, CT, QKW])
        rot_b = sb("rot_b", [P, CT, QKW])
        qsum = sb("qsum", [P, CT * QKH])
        qroot = sb("qroot", [P, CT * QKH])
        qinv = sb("qinv", [P, CT * QKH])
        qn = sb("qn", [P, CT, QKW])
        rest = sb("rest", [P, CT, QKW])
        parts = [sb(f"parts{i}", [P, CT, QKH, ROWS3], BF16) for i in range(2)]
        k_wide = [sb(f"k_wide{i}", [P, CT, KV_HEADS, STACK], BF16) for i in range(2)]
        stats = sb("stats", [P, CT, 6])
        moments = sb("moments", [P, CT, 2])
        zraw = [sb(f"zraw{i}", [P, CT, D]) for i in range(2)]
        qs = [sb(f"qs{i}", [STACK, GROUP, SEQ], BF16) for i in range(2)]
        ks = [sb(f"ks{i}", [STACK, WIN + SEQ], BF16) for i in range(2)]
        wide = sb("wide", [P, 4 * PER_STEP, BANK])
        probs = [wide[:, PER_STEP * i:PER_STEP * (i + 1), :] for i in range(4)]
        h_t = [wide[:, FF // P * i:FF // P * (i + 1), :] for i in range(2)]
        vs = [sb(f"vs{i}", [P, KT, 32]) for i in range(2)]
        v_diag = [[sb(f"v_{n}{i}", [P, KT, P]) for i in range(2)] for n in ("own", "prev")]
        acc_t = [sb(f"acc_t{i}", [P, BANK]) for i in range(2)]
        linv = sb("linv", [P, 4 * GROUP])

        eps_rms, eps_ln = sb("eps_rms", [P, 1]), sb("eps_ln", [P, 1])
        o_t = [sb(f"o_t{i}", [P, CHUNK]) for i in range(2)]
        zn_t = [sb(f"zn_t{i}", [P, CHUNK]) for i in range(2)]
        wsum = sb("wsum", [P, 2])
        gamma_t = sb("gamma", [P, 2])
        sq_x = sb("sq_x", [P, CT, D])
        threshold, minus_threshold = sb("threshold", [P, 2]), sb("minus_threshold", [P, 2])
        y_moments, y_root_t, y_inv = sb("y_moments_t", [P, CT, 2]), sb("y_root_t", [P, CT]), sb("y_inv", [P, CT])

        ps = ctx.enter_context(nc.psum_tensor("ps", [P, 8, BANK], F32))

        x_in = [sem(f"x_in{c}") for c in range(CHUNKS)]
        wts_in = sem("wts_in")
        ffw_in = sem("ffw_in")
        consts = sem("consts")
        dve_c = sem("dve_c")
        act_c = sem("act_c")
        pool_c = sem("pool_c")
        S = {}
        for ph in "gl":
            for n in ("ssum", "sroot", "xs", "xt", "xn", "lat", "latc", "pj", "pjfree", "rot", "sq", "qsum",
                      "qroot", "parts", "kwide", "pt", "qcopied", "kcopied", "ot", "otc", "wo", "x1"):
                S[n + ph] = sem(f"{n}_{ph}")
            for n in ("sdone", "exped", "pfree", "sfree", "accdone", "accfree", "unitfree", "ufreep",
                      "evac", "tdone", "vready", "masked", "linv"):
                S[n + ph] = sem(f"a_{n}_{ph}")
            S["stk0" + ph], S["stk1" + ph] = sem(f"stack_in0_{ph}"), sem(f"stack_in1_{ph}")
        vshift = sem("vshift")
        amax = sem("abs_sums")
        gam = sem("gamma")
        wq_done, wt_done, wtc = sem("w_quantised"), sem("w_transposed"), sem("w_copied")
        z_ready, z_root, zn_ready = sem("z_moments"), sem("z_root"), sem("zn_ready")
        zt, ztc, hmm, hact, ymm = sem("zt"), sem("ztc"), sem("h_mm"), sem("h_act"), sem("y_mm")
        y_m, y_root, y_ready, stored = sem("y_moments"), sem("y_root"), sem("y_ready"), sem("stored")
        zfree = sem("z_bank_free")
        dve_consts = sem("dve_consts")
        gamc = sem("gamma_copied")
        pool_go = sem("pool_go")

        block = ctx.enter_context(nc.Block())

        def chunk_tiles(c):
            return slice(c * CT, (c + 1) * CT)

        def banks(a, n):
            return ps[:, a:a + n, :].rearrange("p a b -> p (a b)")

        WTS = 14 * 16

        @block.sync
        def _(sp):
            for c in range(CHUNKS):
                src = hidden.rearrange("b (t p) d -> p (b t) d", p=P)
                sp.dma_start(x0[:, chunk_tiles(c), :], src[:, chunk_tiles(c), :]).then_inc(x_in[c], 16)
                if c == 0:
                    for dst, s in ((nw[0][:, :], norm1_w.rearrange("(p a) -> p a", a=1)),
                                   (nw[1][:, :], norm2_w.rearrange("(p a) -> p a", a=1)),
                                   (wqkv_g[:, :], g_wq), (wdown[:, :], g_kv_down),
                                   (wup[:, 0:KVW], g_k_up), (wup[:, KVW:2 * KVW], g_v_up),
                                   (rope[:, :, :, :], rope_tab.rearrange("(t p) h c -> p t h c", p=P))):
                        sp.dma_start(dst, s).then_inc(wts_in, 16)
            for dst, s in ((wo[0][:, :], g_wo), (wo[1][:, :], l_wo),
                           (wqkv_l[:, 0:QW], l_wq), (wqkv_l[:, QW:QKW], l_wk),
                           (wqkv_l[:, QKW:QKW + KVW], l_wv),
                           (b2b[:, :], b2.partition_broadcast(P))):
                sp.dma_start(dst, s).then_inc(wts_in, 16)
            sp.dma_start(b1c[:, :], b1.rearrange("(a p) -> p a", p=P), allow_slow_non_contiguous=True)\
                .then_inc(wts_in, 16)
            sp.dma_start(w1n[:, :, :], w1.rearrange("(a p) d -> p a d", p=P)).then_inc(ffw_in, 16)
            sp.dma_start(w2n[:, :], w2).then_inc(ffw_in, 16)

            for ph in "gl":
                sp.wait_ge(S["qcopied" + ph], CHUNKS)
                sp.wait_ge(S["kcopied" + ph], CHUNKS)
                if ph == "l":
                    sp.wait_ge(S["pjfreel"], CHUNKS)
                    sp.wait_ge(consts, 1)
                    sp.dma_start(v_prev[WIN:P, :, :], v_all[0:P - WIN, :, :]).then_inc(vshift, 16)
                    for b in range(BATCH):
                        sp.dma_start(v_prev[0:WIN, b * KT + 1:(b + 1) * KT, :],
                                     v_all[P - WIN:P, b * KT:(b + 1) * KT - 1, :]).then_inc(vshift, 16)
                sp.wait_ge(consts, 1)
                with sp.Fori(0, BATCH) as b, sp.Fori(0, KV_HEADS // 2) as gp:
                    for u in range(2):
                        unit = b * KV_HEADS + gp * 2 + u
                        sp.wait_ge(S["unitfree" + ph], unit + 1)
                        sp.dma_start(ks[u][:, WIN:WIN + SEQ],
                                     k_stacks[:, bass.ds(unit, 1), :].rearrange("p a n -> p (a n)"))\
                            .then_inc(S[f"stk{u}" + ph], 16)
                        for h in range(GROUP):
                            src = q_parts[h * ROWS3:(h + 1) * ROWS3, bass.ds(unit, 1), :]
                            for j in range(PARTS):
                                sp.dma_start(qs[u][j * ROWS3:(j + 1) * ROWS3, h:h + 1, :], src)\
                                    .then_inc(S[f"stk{u}" + ph], 16)

            dst = out.rearrange("b (t p) d -> p (b t) d", p=P)
            for c in range(CHUNKS):
                sp.wait_ge(y_ready, c + 1)
                sp.dma_start(dst[:, chunk_tiles(c), :], x1[:, chunk_tiles(c), :]).then_inc(stored, 16)
            sp.wait_ge(stored, 16 * CHUNKS)

        STACK_DMAS = 16 * (1 + GROUP * PARTS)

        @block.gpsimd
        def _(pool):
            link_n = [0]

            def link(ins):
                link_n[0] += 1
                ins.then_inc(pool_c, 1)
                pool.wait_ge(pool_c, link_n[0])

            nc.gpsimd.memset(ones[:, :], 1.0)
            nc.gpsimd.memset(ident[:, :], 0.0)
            link(nc.gpsimd.memset(ident_bf[:, :], 0.0))
            for m in (ident, ident_bf):
                last = nc.gpsimd.affine_select(out=m[:, :], in_=m[:, :], compare_op=ALU.not_equal, fill=1.0,
                                               base=0, pattern=[[-1, P]], channel_multiplier=1)
            link(last)
            for i in range(2):
                nc.gpsimd.memset(vs[i][:, :, :], 1.0)
                nc.gpsimd.memset(ks[i][:, 0:WIN], 0.0)
                for n in range(2):
                    nc.gpsimd.memset(v_diag[n][i][:, :, :], 0.0)
            nc.gpsimd.memset(v_prev[:, :, :], 0.0)
            link(nc.gpsimd.memset(band[:, :, :, :], 0.0))
            for j in range(P // WIN):
                rows = slice(j * WIN, (j + 1) * WIN)
                half = band[rows, :, 0, :].rearrange("p t (h q) -> p t h q", h=GROUP)
                nc.gpsimd.affine_select(out=half, in_=half, compare_op=ALU.is_ge, fill=MASKED, base=0,
                                        pattern=[[0, 2], [0, GROUP], [1, WIN]], channel_multiplier=-1)
                half = band[rows, :, 1, :].rearrange("p t (h q) -> p t h q", h=GROUP)
                last = nc.gpsimd.affine_select(out=half, in_=half, compare_op=ALU.is_gt, fill=MASKED, base=0,
                                               pattern=[[0, 2], [0, GROUP], [-1, WIN]], channel_multiplier=1)
                for i in range(2):
                    for n in range(2):
                        first = 1 if (n, j) == (1, 0) else 0
                        last = nc.gpsimd.memset(v_diag[n][i][rows, first:, j * WIN + HD:(j + 1) * WIN], 1.0)
            last.then_inc(consts, 1)

            def widen_keys(ph, n):
                for c in range(CHUNKS):
                    pool.wait_ge(S["parts" + ph], c + 1)
                    if c >= 2:
                        pool.wait_ge(S["pt" + ph], c - 1)
                    for t in range(CT):
                        src = parts[c % 2][:, t, HEADS:QKH, :].rearrange("p h (j d) -> p (h j) d", d=HD)
                        dst = k_wide[c % 2][:, t, :, :].rearrange("p h (j i d) -> p (h j) i d", i=PARTS, d=HD)
                        for i in range(PARTS):
                            last = nc.gpsimd.tensor_copy(dst[:, :, i, :], src)
                    last.then_inc(S["kwide" + ph], 1)

            widen_keys("g", 0)
            with pool.Fori(0, BATCH) as b, pool.Fori(0, KV_HEADS // 2) as gp:
                for u in range(2):
                    unit = b * KV_HEADS + gp * 2 + u
                    pool.wait_ge(S["accfreeg"], unit * 2 + 1)
                    src = v_all[:, bass.ds(b * KT, KT), bass.ds((gp * 2 + u) * HD, HD)]
                    nc.gpsimd.tensor_copy(vs[u][:, :, 0:HD], src).then_inc(S["vreadyg"], 1)
                    for s in MASKED_STEPS:
                        pool.wait_ge(S["expedg"], unit * STEPS + s + 1)
                        pool.sem_inc(pool_go, 1)
                        for first, n, cols in diagonal_runs(s):
                            for at in cols:
                                blk = probs[s % 4][:, first:first + n, at:at + P]
                                last = nc.gpsimd.affine_select(out=blk, in_=blk, compare_op=ALU.is_ge, fill=0.0,
                                                               base=0, pattern=[[0, n], [1, P]],
                                                               channel_multiplier=-1)
                        last.then_inc(S["maskedg"], 1)
            widen_keys("l", 1)
            pool.wait_ge(vshift, 16 * (1 + BATCH))
            with pool.Fori(0, BATCH) as b, pool.Fori(0, KV_HEADS // 2) as gp:
                for u in range(2):
                    unit = b * KV_HEADS + gp * 2 + u
                    pool.wait_ge(S["accfreel"], unit * 2 + 1)
                    for n, v in ((0, v_all), (1, v_prev)):
                        for j in range(P // WIN):
                            rows = slice(j * WIN, (j + 1) * WIN)
                            last = nc.gpsimd.tensor_copy(v_diag[n][u][rows, :, j * WIN:j * WIN + HD],
                                                         v[rows, bass.ds(b * KT, KT),
                                                           bass.ds((gp * 2 + u) * HD, HD)])
                    last.then_inc(S["vreadyl"], 1)

        @block.scalar
        def _(act):
            def front(ph, c):
                n = "gl".index(ph)
                if ph == "l":
                    act.wait_ge(S["otg"], c + 1)
                    if c >= 2:
                        act.wait_ge(S["wog"], c - 1)
                    nc.scalar.activation(o_t[c % 2][:, :], ps[:, 0, :], ACT.Copy).then_inc(S["otcg"], 1)
                act.wait_ge(S["ssum" + ph], c + 1)
                nc.scalar.activation(sroot[:, :], ssum[:, :], ACT.Sqrt, bias=eps_rms[:, :], scale=1.0 / D)\
                    .then_inc(S["sroot" + ph], 1)
                act.wait_ge(S["xt" + ph], c + 1)
                nc.scalar.activation(xn_t[c % 2][:, :], ps[:, 0, :], ACT.Copy, scale=nw[n][:, :])\
                    .then_inc(S["xn" + ph], 1)
                if ph == "g":
                    act.wait_ge(S["latg"], c + 1)
                    nc.scalar.activation(lat_t[c % 2][:, :], ps[0:LATENT, 1, :], ACT.Copy)\
                        .then_inc(S["latcg"], 1)

            def back(ph, c):
                act.wait_ge(S["rot" + ph], c + 1)
                nc.scalar.activation(sq[:, :, :], rot[:, :, :], ACT.Square).then_inc(S["sq" + ph], 1)
                act.wait_ge(S["qsum" + ph], c + 1)
                nc.scalar.activation(qroot[:, :], qsum[:, :], ACT.Sqrt, bias=eps_rms[:, :], scale=1.0 / HD)\
                    .then_inc(S["qroot" + ph], 1)

            def copy_q(ph, c):
                act.wait_ge(S["pt" + ph], c + 1)
                b, at = c // 2, (c % 2) * CHUNK
                src = banks(4, 2).bitcast(BF16)[0:GROUP * ROWS3, :].rearrange("p (g n) -> p g n", g=KV_HEADS)
                nc.scalar.activation(q_parts[:, b * KV_HEADS:(b + 1) * KV_HEADS, at:at + CHUNK], src, ACT.Copy)\
                    .then_inc(S["qcopied" + ph], 1)

            def project(ph):
                front(ph, 0)
                for c in range(CHUNKS):
                    if c + 1 < CHUNKS:
                        front(ph, c + 1)
                    if c >= 1:
                        copy_q(ph, c - 1)
                    back(ph, c)
                copy_q(ph, CHUNKS - 1)

            act.wait_ge(dve_consts, 1)
            act.wait_ge(wts_in, WTS)
            act.wait_ge(ffw_in, 32)
            nc.scalar.activation(zraw[0][:, :, :], w1n[:, :, :], ACT.Abs,
                                 accum_out=wsum[:, 0:1])
            nc.scalar.activation(zraw[1][:, :, :].rearrange("p a d -> p (a d)"), w2n[:, :], ACT.Abs, accum_out=wsum[:, 1:2]).then_inc(amax, 1)
            project("g")

            with act.Fori(0, BATCH) as b, act.Fori(0, KV_HEADS // 2) as gp:
                for u in range(2):
                    step0 = (b * KV_HEADS + gp * 2 + u) * STEPS
                    for s in range(STEPS):
                        act.wait_ge(S["sdoneg"], step0 + s + 1)
                        act.wait_ge(S["pfreeg"], step0 + s + 1)
                        slot = (s % 2) * PER_STEP
                        nc.scalar.activation(probs[s % 4][:, :, :], ps[:, slot:slot + PER_STEP, :], ACT.Exp,
                                             scale=SCALE).then_inc(S["expedg"], 1)
            project("l")
            act.sem_inc(S["expedl"], 1)
            with act.Fori(0, BATCH) as b, act.Fori(0, KV_HEADS // 2) as gp:
                for u in range(2):
                    step0 = (b * KV_HEADS + gp * 2 + u) * LOCAL_STEPS
                    for s in range(LOCAL_STEPS):
                        act.wait_ge(S["sdonel"], step0 + s + 1)
                        act.wait_ge(S["pfreel"], step0 + s + 1)
                        nc.scalar.activation(probs[s][:, 0:2, :], ps[:, 2 * s:2 * s + 2, :], ACT.Exp,
                                             scale=SCALE).then_inc(S["expedl"], 1)

            def tail_front(c):
                act.wait_ge(S["otl"], c + 1)
                if c >= 2:
                    act.wait_ge(S["wol"], c - 1)
                nc.scalar.activation(o_t[c % 2][:, :], ps[:, 0, :], ACT.Copy).then_inc(S["otcl"], 1)
                act.wait_ge(z_ready, c + 1)
                nc.scalar.activation(sroot[:, :], moments[:, :, 1], ACT.Sqrt, bias=eps_ln[:, :]).then_inc(z_root, 1)
                act.wait_ge(zt, c + 1)
                nc.scalar.activation(zn_t[c % 2][:, :], ps[:, 2, :], ACT.Copy)\
                    .then_inc(ztc, 1)

            def tail_back(c):
                for f in range(FF // P):
                    act.wait_ge(hmm, c * (FF // P) + f + 1)
                    nc.scalar.activation(h_t[c % 2][:, f, :], ps[:, 3 + f, :], ACT.Relu, bias=b1c[:, f:f + 1])\
                        .then_inc(hact, 1)
                act.wait_ge(y_m, c + 1)
                nc.scalar.activation(y_root_t[:, :], y_moments[:, :, 1], ACT.Sqrt, bias=eps_ln[:, :]).then_inc(y_root, 1)

            tail_front(0)
            for c in range(CHUNKS):
                if c + 1 < CHUNKS:
                    tail_front(c + 1)
                tail_back(c)

        @block.vector
        def _(dve):
            link_n = [0]

            def link(ins):
                link_n[0] += 1
                ins.then_inc(dve_c, 1)
                dve.wait_ge(dve_c, link_n[0])

            def front(ph, c):
                x = x0
                if ph == "g":
                    dve.wait_ge(x_in[c], 16)
                else:
                    dve.wait_ge(S["wog"], c + 1)
                    ins = nc.vector.tensor_tensor(x1[:, chunk_tiles(c), :], x0[:, chunk_tiles(c), :],
                                                  ps[:, 1, :].rearrange("p (t d) -> p t d", d=D), ALU.add)
                    ins.then_inc(S["x1g"], 1)
                    dve.wait_ge(S["x1g"], c + 1)
                    x = x1
                link(nc.vector.tensor_tensor(sq_x[:, :, :], x[:, chunk_tiles(c), :], x[:, chunk_tiles(c), :], ALU.mult))
                nc.vector.reduce_sum(ssum[:, :], sq_x[:, :, :], AX.X).then_inc(S["ssum" + ph], 1)
                dve.wait_ge(S["sroot" + ph], c + 1)
                link(nc.vector.reciprocal(sinv[:, :], sroot[:, :]))
                if c >= 2:
                    dve.wait_ge(S["xt" + ph], c - 1)
                nc.vector.tensor_tensor(xs[c % 2][:, :, :], x[:, chunk_tiles(c), :],
                                        sinv[:, :].unsqueeze(2).broadcast_to([P, CT, D]), ALU.mult)\
                    .then_inc(S["xs" + ph], 1)

            def back(ph, c):
                n = "gl".index(ph)
                kt0 = (c % 2) * CT
                pj = banks(2, 2).rearrange("p (t f) -> p t f", f=256)
                dve.wait_ge(S["pj" + ph], c + 1)
                nc.vector.tensor_copy(v_all[:, chunk_tiles(c), :], pj[:, :, QKW:QKW + KVW])
                cos = rope[:, kt0:kt0 + CT, n, 0:HD].unsqueeze(2).broadcast_to([P, CT, QKH, HD])
                nc.vector.tensor_tensor(rot[:, :, :].rearrange("p t (h d) -> p t h d", d=HD),
                                        pj[:, :, 0:QKW].rearrange("p t (h d) -> p t h d", d=HD), cos, ALU.mult)
                for odd in range(2):
                    sin = rope[:, kt0:kt0 + CT, n, HD + odd * HD // 2:HD + (odd + 1) * HD // 2]
                    sin = sin.unsqueeze(2).broadcast_to([P, CT, QKH, HD // 2])
                    dst = rot_b[:, :, :].rearrange("p t (h e o) -> p t h e o", e=HD // 2, o=2)[:, :, :, :, odd]
                    src = pj[:, :, 0:QKW].rearrange("p t (h e o) -> p t h e o", e=HD // 2, o=2)[:, :, :, :, 1 - odd]
                    ins = nc.vector.tensor_tensor(dst, src, sin, ALU.mult)
                ins.then_inc(S["pjfree" + ph], 1)
                dve.wait_ge(S["pjfree" + ph], c + 1)
                nc.vector.tensor_tensor(rot[:, :, :], rot[:, :, :], rot_b[:, :, :], ALU.add)\
                    .then_inc(S["rot" + ph], 1)
                dve.wait_ge(S["sq" + ph], c + 1)
                heads = "p t (h d) -> p (t h) d"
                nc.vector.reduce_sum(qsum[:, :], sq[:, :, :].rearrange(heads, d=HD), AX.X)\
                    .then_inc(S["qsum" + ph], 1)
                dve.wait_ge(S["qroot" + ph], c + 1)
                link(nc.vector.reciprocal(qinv[:, :], qroot[:, :]))
                link(nc.vector.tensor_tensor(qn[:, :, :].rearrange(heads, d=HD), rot[:, :, :].rearrange(heads, d=HD),
                                             qinv[:, :].unsqueeze(2).broadcast_to([P, CT * QKH, HD]), ALU.mult))
                if c >= 2:
                    dve.wait_ge(S["pt" + ph], c - 1)
                part = [parts[c % 2][:, :, :, i * HD:(i + 1) * HD].rearrange("p t h d -> p (t h) d")
                        for i in range(PARTS)]
                full, left = qn[:, :, :].rearrange(heads, d=HD), rest[:, :, :].rearrange(heads, d=HD)
                link(nc.vector.tensor_copy(part[0], full))
                link(nc.vector.tensor_tensor(left, full, part[0], ALU.subtract))
                link(nc.vector.tensor_copy(part[1], left))
                nc.vector.tensor_tensor(part[2], left, part[1], ALU.subtract).then_inc(S["parts" + ph], 1)

            def copy_k(ph, c):
                dve.wait_ge(S["pt" + ph], c + 1)
                b, at = c // 2, (c % 2) * CHUNK
                src = banks(6, 2).bitcast(BF16)[0:STACK, :].rearrange("p (g n) -> p g n", g=KV_HEADS)
                nc.vector.tensor_copy(k_stacks[:, b * KV_HEADS:(b + 1) * KV_HEADS, at:at + CHUNK], src)\
                    .then_inc(S["kcopied" + ph], 1)

            def project(ph):
                front(ph, 0)
                for c in range(CHUNKS):
                    if c + 1 < CHUNKS:
                        front(ph, c + 1)
                    if c >= 1:
                        copy_k(ph, c - 1)
                    back(ph, c)
                copy_k(ph, CHUNKS - 1)

            nc.vector.memset(eps_rms[:, :], EPS_RMS)
            nc.vector.memset(eps_ln[:, :], EPS_LN).then_inc(dve_consts, 1)
            dve.wait_ge(gam, 1)
            nc.vector.tensor_scalar(gamma_t[:, :], ps[:, 7, 0:2], 1.0 / (FF * D), EPS_Q, ALU.mult, ALU.add)\
                .then_inc(gamc, 1)
            dve.wait_ge(gamc, 1)
            dve.wait_ge(wts_in, WTS)
            project("g")

            link(nc.vector.tensor_scalar(threshold[:, :], gamma_t[:, :], 0.5, None, ALU.mult))
            link(nc.vector.tensor_scalar(minus_threshold[:, :], threshold[:, :], -1.0, None, ALU.mult))
            for i, w in ((0, w1n[:, :, :].rearrange("p a d -> p (a d)")), (1, w2n[:, :])):
                low = zraw[i][:, :, :].rearrange("p a d -> p (a d)")
                link(nc.vector.tensor_scalar(low, w, minus_threshold[:, i:i + 1], None, ALU.is_lt))
                ins = nc.vector.scalar_tensor_tensor(out=w, in0=w, scalar=threshold[:, i:i + 1],
                                                     in1=low, op0=ALU.is_gt, op1=ALU.subtract)
            ins.then_inc(wq_done, 1)
            dve.wait_ge(wt_done, 1)
            nc.vector.tensor_copy(w1q[:, :], ps[:, 6, :])
            nc.vector.tensor_copy(w2q[:, :, :].rearrange("p a d -> p (a d)"), ps[:, 7, :]).then_inc(wtc, 1)

            with dve.Fori(0, BATCH) as b, dve.Fori(0, KV_HEADS // 2) as gp:
                for u in range(2):
                    unit = b * KV_HEADS + gp * 2 + u
                    for qc in range(2):
                        if qc == 0:
                            dve.wait_ge(S["accdoneg"], unit + 1)
                        else:
                            dve.wait_ge(S["pfreeg"], 4 + (unit + 1) * STEPS)
                        nc.vector.tensor_copy(acc_t[qc][:, :], ps[:, 6 + qc, :]).then_inc(S["evacg"], 1)
                        dve.wait_ge(S["tdoneg"], unit * 2 + qc + 1)
                        o = ps[:, 6 + qc, :].rearrange("p (t h c) -> p t h c", t=CT, c=32)
                        nc.vector.reciprocal(linv[:, :].rearrange("p (t h) -> p t h", h=GROUP), o[:, :, :, HD])\
                            .then_inc(S["linvg"], 1)
                        dve.wait_ge(S["linvg"], unit * 2 + qc + 1)
                        dst = heads_out[:, bass.ds(b * KT + qc * CT, CT), bass.ds((gp * 2 + u) * GROUP * HD, GROUP * HD)]
                        nc.vector.tensor_tensor(dst.rearrange("p t (h d) -> p t h d", d=HD), o[:, :, :, 0:HD],
                                                linv[:, :].rearrange("p (t h) -> p t h", h=GROUP).unsqueeze(3)
                                                .broadcast_to([P, CT, GROUP, HD]), ALU.mult)\
                            .then_inc(S["accfreeg"], 1)
            project("l")
            with dve.Fori(0, BATCH) as b, dve.Fori(0, KV_HEADS // 2) as gp:
                for u in range(2):
                    for s in range(LOCAL_STEPS):
                        step = (b * KV_HEADS + gp * 2 + u) * LOCAL_STEPS + s
                        dve.wait_ge(S["pfreel"], 2 + step + 1)
                        nc.vector.transpose(acc_t[s][:, :], ps[:, 6 + s, :]).then_inc(S["accfreel"], 1)
                        dve.wait_ge(S["accfreel"], step + 3)
                        o = acc_t[s][:, :].rearrange("p (t h c) -> p t h c", t=CT, c=32)
                        nc.vector.reciprocal(linv[:, :].rearrange("p (t h) -> p t h", h=GROUP), o[:, :, :, HD])\
                            .then_inc(S["linvl"], 1)
                        dve.wait_ge(S["linvl"], step + 1)
                        dst = heads_out[:, bass.ds(b * KT + s * CT, CT), bass.ds((gp * 2 + u) * GROUP * HD, GROUP * HD)]
                        nc.vector.tensor_tensor(dst.rearrange("p t (h d) -> p t h d", d=HD), o[:, :, :, 0:HD],
                                                linv[:, :].rearrange("p (t h) -> p t h", h=GROUP).unsqueeze(3)
                                                .broadcast_to([P, CT, GROUP, HD]), ALU.mult)\
                            .then_inc(S["tdonel"], 1)

            def layer_norm_stats(z, moments_t):
                for t in range(CT):
                    ins = nc.vector.bn_stats(stats[:, t, :], z[:, t, :])
                link(ins)
                for t in range(CT):
                    ins = nc.vector.bn_aggr(moments_t[:, t, :], stats[:, t, :])
                return ins

            def tail_front(c):
                z = zraw[c % 2]
                if c >= 2:
                    dve.wait_ge(y_ready, c - 1)
                dve.wait_ge(S["wol"], c + 1)
                nc.vector.tensor_tensor(z[:, :, :], x1[:, chunk_tiles(c), :],
                                        ps[:, 1, :].rearrange("p (t d) -> p t d", d=D), ALU.add).then_inc(zfree, 1)
                dve.wait_ge(zfree, c + 1)
                link(nc.vector.tensor_tensor(z[:, :, :], z[:, :, :], x0[:, chunk_tiles(c), :], ALU.add))
                layer_norm_stats(z, moments).then_inc(z_ready, 1)
                dve.wait_ge(z_root, c + 1)
                link(nc.vector.reciprocal(sinv[:, :], sroot[:, :]))
                if c >= 2:
                    dve.wait_ge(zt, c - 1)
                for t in range(CT):
                    ins = nc.vector.tensor_scalar(xs[c % 2][:, t, :], z[:, t, :], moments[:, t, 0:1],
                                                  sinv[:, t:t + 1], ALU.subtract, ALU.mult)
                ins.then_inc(zn_ready, 1)

            def tail_back(c):
                y = zraw[c % 2]
                dve.wait_ge(ymm, c + 1)
                link(nc.vector.tensor_tensor(y[:, :, :], ps[:, 7, :].rearrange("p (t d) -> p t d", d=D),
                                             b2b[:, :].unsqueeze(1).broadcast_to([P, CT, D]), ALU.add))
                link(nc.vector.tensor_tensor(y[:, :, :], y[:, :, :], xs[c % 2][:, :, :], ALU.add))
                layer_norm_stats(y, y_moments).then_inc(y_m, 1)
                dve.wait_ge(y_root, c + 1)
                link(nc.vector.reciprocal(y_inv[:, :], y_root_t[:, :]))
                for t in range(CT):
                    ins = nc.vector.tensor_scalar(x1[:, c * CT + t, :], y[:, t, :], y_moments[:, t, 0:1],
                                                  y_inv[:, t:t + 1], ALU.subtract, ALU.mult)
                ins.then_inc(y_ready, 1)

            tail_front(0)
            for c in range(CHUNKS):
                if c + 1 < CHUNKS:
                    tail_front(c + 1)
                tail_back(c)

        @block.tensor
        def _(pe):
            def transposes(bank, src):
                for t in range(CT):
                    ins = nc.tensor.transpose(ps[:, bank, t * P:(t + 1) * P], src(t), ident[:, :])
                return ins

            def output_projection(ph, c):
                transposes(0, lambda t: heads_out[:, c * CT + t, :]).then_inc(S["ot" + ph], 1)
                pe.wait_ge(S["otc" + ph], c + 1)
                for t in range(CT):
                    ins = nc.tensor.matmul(ps[:, 1, t * P:(t + 1) * P], o_t[c % 2][:, t * P:(t + 1) * P],
                                           wo["gl".index(ph)][:, :], start=True, stop=True)
                ins.then_inc(S["wo" + ph], 1)

            def front(ph, c):
                if ph == "l":
                    if c >= 1:
                        pe.wait_ge(S["xnl"], c)
                        pe.wait_ge(S["x1g"], c)
                    output_projection("g", c)
                elif c >= 1:
                    pe.wait_ge(S["xng"], c)
                pe.wait_ge(S["xs" + ph], c + 1)
                transposes(0, lambda t: xs[c % 2][:, t, :]).then_inc(S["xt" + ph], 1)
                pe.wait_ge(S["xn" + ph], c + 1)
                xn = xn_t[c % 2]
                if ph == "g":
                    nc.tensor.matmul(ps[0:LATENT, 1, :], wdown[:, :], xn[:, :], start=True, stop=True)\
                        .then_inc(S["latg"], 1)
                if c >= 1:
                    pe.wait_ge(S["pjfree" + ph], c)
                if ph == "g":
                    pe.wait_ge(S["latcg"], c + 1)
                for t in range(CT):
                    tok = slice(t * P, (t + 1) * P)
                    to = ps[:, 2 + t // 2, (t % 2) * 256:(t % 2) * 256 + QKW + KVW]
                    if ph == "g":
                        nc.tensor.matmul(to[:, 0:QW], xn[:, tok], wqkv_g[:, :], start=True, stop=True)
                        ins = nc.tensor.matmul(to[:, QW:QKW + KVW], lat_t[c % 2][:, tok], wup[:, :],
                                               start=True, stop=True)
                    else:
                        ins = nc.tensor.matmul(to, xn[:, tok], wqkv_l[:, :], start=True, stop=True)
                ins.then_inc(S["pj" + ph], 1)

            def back(ph, c):
                if c >= 1:
                    pe.wait_ge(S["qcopied" + ph], c)
                    pe.wait_ge(S["kcopied" + ph], c)
                pe.wait_ge(S["parts" + ph], c + 1)
                q_out, k_out = banks(4, 2).bitcast(BF16), banks(6, 2).bitcast(BF16)
                for t in range(CT):
                    for g in range(KV_HEADS):
                        at = g * CHUNK + t * P
                        src = parts[c % 2][:, t, g * GROUP:(g + 1) * GROUP, :].rearrange("p h r -> p (h r)")
                        nc.tensor.transpose(q_out[0:GROUP * ROWS3, at:at + P], src, ident_bf[:, :])
                pe.wait_ge(S["kwide" + ph], c + 1)
                for t in range(CT):
                    for g in range(KV_HEADS):
                        at = g * CHUNK + t * P
                        ins = nc.tensor.transpose(k_out[0:STACK, at:at + P], k_wide[c % 2][:, t, g, :], ident_bf[:, :])
                ins.then_inc(S["pt" + ph], 1)

            def project(ph):
                front(ph, 0)
                for c in range(CHUNKS):
                    if c + 1 < CHUNKS:
                        front(ph, c + 1)
                    back(ph, c)

            def scores(u, s, pair, step):
                if s == 0:
                    pe.wait_ge(S[f"stk{u}g"], (pair + 1) * STACK_DMAS)
                for n in range(PER_STEP):
                    at = 0
                    for h, kt, q0, w in FILLS[PER_STEP * s + n]:
                        ins = nc.tensor.matmul(ps[:, (s % 2) * PER_STEP + n, at:at + w],
                                               ks[u][:, WIN + kt * P:WIN + (kt + 1) * P], qs[u][:, h, q0:q0 + w],
                                               start=True, stop=True)
                        at += w
                ins.then_inc(S["sdoneg"], 1)

            def weighted(u, s, unit):
                if s == 0:
                    pe.wait_ge(S["vreadyg"], unit + 1)
                pe.wait_ge(S["expedg"], unit * STEPS + s + 1)
                if s in MASKED_STEPS:
                    pe.wait_ge(S["maskedg"], unit * len(MASKED_STEPS) + MASKED_STEPS.index(s) + 1)
                first_head = FILLS[PER_STEP * s][0][0]
                for n in range(PER_STEP):
                    fill, at = PER_STEP * s + n, 0
                    qc = int(fill >= FILLS_QC0)
                    if fill in (0, FILLS_QC0):
                        pe.wait_ge(S["accfreeg"], unit * 2 + qc + 1)
                    for h, kt, q0, w in FILLS[fill]:
                        to = q0 - qc * CHUNK
                        last = kt == (qc + 1) * CT - 2
                        ins = nc.tensor.matmul(ps[32 * h:32 * h + 32, 6 + qc, to:to + w], vs[u][:, kt, :],
                                               probs[s % 4][:, n, at:at + w], start=kt == 0, stop=last)
                        if s == STEPS - 3 and n == 0 and at == 0 and h == first_head:
                            ins.then_inc(S["unitfreeg"], 1)
                        at += w
                    if fill == FILLS_QC0 - 1:
                        ins.then_inc(S["accdoneg"], 1)
                ins.then_inc(S["pfreeg"], 1)

            def to_tokens(qc, unit):
                pe.wait_ge(S["evacg"], unit * 2 + qc + 1)
                transposes(6 + qc, lambda t: acc_t[qc][:, t * P:(t + 1) * P]).then_inc(S["tdoneg"], 1)

            pe.wait_ge(consts, 1)
            pe.wait_ge(wts_in, WTS)
            pe.wait_ge(amax, 1)
            nc.tensor.matmul(ps[:, 7, 0:2], ones[:, :], wsum[:, :], start=True, stop=True).then_inc(gam, 1)
            pe.wait_ge(gamc, 1)
            project("g")
            pe.wait_ge(S["kcopiedg"], CHUNKS)
            pe.wait_ge(wq_done, 1)
            transposes(6, lambda t: w1n[:, t, :])
            transposes(7, lambda t: w2n[:, t * P:(t + 1) * P]).then_inc(wt_done, 1)

            pe.sem_inc(S["unitfreeg"], 2)
            pe.sem_inc(S["pfreeg"], 4)
            pe.sem_inc(S["accfreeg"], 2)
            pe.wait_ge(S["qcopiedg"], CHUNKS)
            scores(0, 0, 0, 0)
            scores(0, 1, 0, 1)
            pe.wait_ge(wtc, 1)
            with pe.Fori(0, BATCH) as b, pe.Fori(0, KV_HEADS // 2) as gp:
                pair = b * (KV_HEADS // 2) + gp
                for u in range(2):
                    unit = b * KV_HEADS + gp * 2 + u
                    for s in range(STEPS):
                        pe.wait_ge(S["expedg"], unit * STEPS + s + 1)
                        if s + 2 < STEPS:
                            scores(u, s + 2, pair, None)
                        elif u == 0:
                            scores(1, s + 2 - STEPS, pair, None)
                        else:
                            with pe.If(pair < UNITS // 2 - 1):
                                scores(0, s + 2 - STEPS, pair + 1, None)
                        weighted(u, s, unit)
                        if s == 5:
                            to_tokens(0, unit)
                        if s == 1 and u == 1:
                            to_tokens(1, unit - 1)
                to_tokens(1, unit)
            pe.wait_ge(S["accfreeg"], 2 + 2 * UNITS)
            project("l")

            def local_scores(u, s, pair):
                if s == 0:
                    pe.wait_ge(S[f"stk{u}l"], (pair + 1) * STACK_DMAS)
                for n in range(2):
                    bank = 2 * s + n
                    nc.tensor.matmul(ps[:, bank, :], ident_bf[:, :], band[:, :, :, :].rearrange("p a b c -> p (a b c)"),
                                     start=True, stop=False, skip_group_check=True)
                    for k2 in range(2):
                        for half in range(2):
                            for j in range(P // WIN):
                                c = ((4 * s + 2 * n + k2) * P + j * WIN)
                                first = WIN + c if half == 0 else c
                                col = (k2 * 2 + half) * P
                                ins = nc.tensor.matmul(ps[WIN * j:WIN * (j + 1), bank, col:col + P],
                                                       ks[u][:, first:first + WIN], qs[u][:, :, c:c + WIN],
                                                       start=False, stop=(k2 == 1 and half == 1), skip_group_check=True)
                ins.then_inc(S["sdonel"], 1)

            def local_weighted(u, s, unit):
                pe.wait_ge(S["expedl"], unit * LOCAL_STEPS + s + 2)
                pe.wait_ge(S["accfreel"], unit * LOCAL_STEPS + s + 1)
                if s == 0:
                    pe.wait_ge(S["vreadyl"], unit + 1)
                for t in range(CT):
                    for half in range(2):
                        ins = nc.tensor.matmul(ps[:, 6 + s, t * P:(t + 1) * P], v_diag[half][u][:, s * CT + t, :],
                                               probs[s][:, t // 2, ((t % 2) * 2 + half) * P:((t % 2) * 2 + half + 1) * P],
                                               start=half == 0, stop=half == 1)
                        if s == 0 and t == half == 0:
                            ins.then_inc(S["unitfreel"], 1)
                ins.then_inc(S["pfreel"], 1)

            pe.sem_inc(S["unitfreel"], 2)
            pe.sem_inc(S["pfreel"], 2)
            pe.sem_inc(S["accfreel"], 2)
            pe.wait_ge(S["kcopiedl"], CHUNKS)
            local_scores(0, 0, 0)
            with pe.Fori(0, BATCH) as b, pe.Fori(0, KV_HEADS // 2) as gp:
                pair = b * (KV_HEADS // 2) + gp
                for u in range(2):
                    unit = b * KV_HEADS + gp * 2 + u
                    for s in range(LOCAL_STEPS):
                        pe.wait_ge(S["expedl"], unit * LOCAL_STEPS + s + 1)
                        if s == 0:
                            local_scores(u, 1, pair)
                        elif u == 0:
                            local_scores(1, 0, pair)
                        else:
                            with pe.If(pair < UNITS // 2 - 1):
                                local_scores(0, 0, pair + 1)
                        local_weighted(u, s, unit)
            pe.wait_ge(S["tdonel"], UNITS * LOCAL_STEPS)

            def tail_front(c):
                if c >= 1:
                    pe.wait_ge(S["otcl"], c)
                    pe.wait_ge(zfree, c)
                output_projection("l", c)
                pe.wait_ge(zn_ready, c + 1)
                if c >= 1:
                    pe.wait_ge(ztc, c)
                transposes(2, lambda t: xs[c % 2][:, t, :]).then_inc(zt, 1)

            def tail_back(c):
                pe.wait_ge(ztc, c + 1)
                for f in range(FF // P):
                    if c >= 1:
                        pe.wait_ge(hact, (c - 1) * (FF // P) + f + 1)
                    nc.tensor.matmul(ps[:, 3 + f, :], w1q[:, f * P:(f + 1) * P], zn_t[c % 2][:, :],
                                     start=True, stop=True).then_inc(hmm, 1)
                pe.wait_ge(hact, (c + 1) * (FF // P))
                if c >= 1:
                    pe.wait_ge(y_m, c)
                for t in range(CT):
                    for f in range(FF // P):
                        ins = nc.tensor.matmul(ps[:, 7, t * P:(t + 1) * P], h_t[c % 2][:, f, t * P:(t + 1) * P],
                                               w2q[:, f, :], start=f == 0, stop=f == FF // P - 1)
                ins.then_inc(ymm, 1)

            tail_front(0)
            for c in range(CHUNKS):
                if c + 1 < CHUNKS:
                    tail_front(c + 1)
                tail_back(c)
    return nc


_INS = ["L0_attn_hidden", "L0_attn_norm1_w", "L0_attn_norm2_w", "L0_attn_g_wq", "L0_attn_g_kv_down",
        "L0_attn_g_k_up", "L0_attn_g_v_up", "L0_attn_g_wo", "L0_attn_l_wq", "L0_attn_l_wk", "L0_attn_l_wv",
        "L0_attn_l_wo", "L0_ffn_W1", "L0_ffn_b1", "L0_ffn_W2", "L0_ffn_b2"]


def rope_table():
    tab = np.zeros((SEQ, 2, 2 * HD), np.float32)
    for n, base in enumerate(BASES):
        inv = np.float32(1.0) / np.float32(base) ** (np.arange(0, HD, 2, dtype=np.float32) / np.float32(HD))
        angle = np.arange(SEQ, dtype=np.float32)[:, None] * inv[None, :].astype(np.float32)
        tab[:, n, 0:HD] = np.repeat(np.cos(angle), 2, axis=1)
        tab[:, n, HD:HD + HD // 2] = -np.sin(angle)
        tab[:, n, HD + HD // 2:] = np.sin(angle)
    return tab


def kernel(**inputs):
    import numpy as _np
    import concourse.bacc as _bacc
    from concourse import mybir as _mybir
    from concourse.bass_utils import run_bass_kernel_spmd as _run

    nc = _bacc.Bacc("TRN2", target_bir_lowering=False, num_devices=1)
    arrays, args = {}, []
    for name in _INS:
        a = _np.ascontiguousarray(inputs[name])
        arrays[f"in_{name}"] = a
        args.append(nc.dram_tensor(f"in_{name}", a.shape, _mybir.dt.from_np(a.dtype), kind="ExternalInput").ap())
    tab = rope_table()
    arrays["in_rope"] = tab
    args.append(nc.dram_tensor("in_rope", tab.shape, _mybir.dt.from_np(tab.dtype), kind="ExternalInput").ap())
    out = nc.dram_tensor("out_0", (BATCH, SEQ, D), _mybir.dt.float32, kind="ExternalOutput").ap()
    build(nc, *args, out)
    r = _run(nc, [arrays], core_ids=[0])
    return r.results[0]["out_0"]
```

```python
from contextlib import ExitStack

import numpy as np

import concourse.bass as bass
from concourse import mybir

BATCH, SEQ, D = 2, 1024, 128
HEADS, KV_HEADS, HD, LATENT, WIN = 16, 4, 8, 32, 32
GROUP = HEADS // KV_HEADS
FF = 4 * D
P = 128
TILES = BATCH * SEQ // P
KT = SEQ // P
CT = 4
CHUNK = CT * P
CHUNKS = TILES // CT
UNITS = BATCH * KV_HEADS
QW, KVW = HEADS * HD, KV_HEADS * HD
QKW = QW + KVW
QKH = HEADS + KV_HEADS
PARTS = 3
ROWS3 = PARTS * HD
STACK = PARTS * ROWS3
BANK = 512
SCALE = float(1.0 / np.sqrt(np.float32(HD)))
BASES = (1000000.0, 10000.0)
EPS_RMS, EPS_LN, EPS_Q = 1e-6, 1e-5, 1e-5
MASKED = -1e30


def score_fills():
    fills = []
    for qc in range(SEQ // CHUNK):
        lo = qc * CHUNK
        first = lo // P
        for kt in range(first + 1):
            fills += [[(h, kt, lo, CHUNK)] for h in range(GROUP)]
        fills += [[(h, first + 1, lo + P, CHUNK - P), (h, first + 3, lo + 3 * P, P)] for h in range(GROUP)]
        fills += [[(h, first + 2, lo + 2 * P, 2 * P), (h + 1, first + 2, lo + 2 * P, 2 * P)]
                  for h in range(0, GROUP, 2)]
    return fills


FILLS = score_fills()
PER_STEP = 3
STEPS = len(FILLS) // PER_STEP
FILLS_QC0 = 10
assert len(FILLS) == STEPS * PER_STEP
RING = 4


def value_groups():
    groups, found = {}, {}
    for f, fill in enumerate(FILLS):
        at = 0
        for h, kt, q0, w in fill:
            found.setdefault((f >= FILLS_QC0, kt), []).append((h, kt, q0, w, f, at))
            at += w
    for (qc, kt), pieces in found.items():
        step = min(max(p[4] for p in pieces) // PER_STEP + 1, STEPS - 1)
        groups.setdefault(step, []).append((int(qc), pieces))
    return groups


GROUPS = value_groups()


LAST_QC0 = max(step for step, groups in GROUPS.items() if any(qc == 0 for qc, _ in groups))


def slots_freed():
    last_use = {}
    for step, groups in GROUPS.items():
        for _, pieces in groups:
            for p in pieces:
                s = p[4] // PER_STEP
                last_use[s] = max(last_use.get(s, 0), step)
    freed, done = {}, 0
    for step in range(STEPS):
        n = 0
        while done < STEPS and last_use[done] <= step:
            done, n = done + 1, n + 1
        freed[step] = n
    return freed


FREED = slots_freed()


def diagonal_runs(step):
    runs = []
    for n in range(PER_STEP):
        at, cols = 0, []
        for _, kt, q0, w in FILLS[PER_STEP * step + n]:
            if kt * P == q0:
                cols.append(at)
            at += w
        if cols and runs and runs[-1][2] == cols and runs[-1][0] + runs[-1][1] == n:
            runs[-1][1] += 1
        elif cols:
            runs.append([n, 1, cols])
    return runs


MASKED_STEPS = [s for s in range(STEPS) if diagonal_runs(s)]
LOCAL_STEPS = 2

NEWTON = 3 + 3 * 3
ADDS = {
    "ocur": {"ocur": 1}, "O": {"use": 1}, "W": {"use": 1}, "F": {"link": 2 + NEWTON, "xs": 1},
    "X": {"use": 1}, "L": {"use": 1}, "P0": {"use": 1, "link": 1}, "P1": {"use": 1, "link": 1},
    "N1": {"link": 3 + NEWTON}, "N2": {"link": 3, "parts": 1},
    "K": {"use": 1}, "Q0": {"use": 1}, "Q1": {"use": 1},
    "Z": {"link": 3 + NEWTON, "xs": 1}, "H0": {"use": 1}, "H1": {"use": 1}, "H2": {"use": 1},
    "H3": {"use": 1}, "Y": {"use": 1, "link": 3 + NEWTON, "y": 1},
    "gamma": {"use": 1, "link": 5}, "wt1": {"use": 1}, "wt2": {"use": 1},
    "tok": {"use": 1, "link": 1},
}


class Item:

    def __init__(self, kind, chain=None, **more):
        self.kind, self.chain, self.counts = kind, chain, {}
        self.step = more.get("step")
        self.unit = more.get("unit")
        self.qc = more.get("qc")
        self.bank = more.get("bank", chain.bank if chain else None)
        if chain:
            chain.items[kind] = self


class Chain:

    def __init__(self, what, bank, batch, half, copies):
        self.what, self.bank, self.batch, self.copies = what, bank, batch, copies
        self.half = half
        self.items = {}


def count_up(plan, so_far, times):
    per, seen = {}, {}
    for item in plan:
        for key, n in ADDS.get(item.kind, {}).items():
            per[item.bank, key] = per.get((item.bank, key), 0) + n
    for item in plan:
        for key, n in ADDS.get(item.kind, {}).items():
            at = (item.bank, key)
            seen[at] = seen.get(at, 0) + n
            item.counts[key] = (so_far.get(at, 0), per[at] if times > 1 else 0, seen[at])
    for at, n in per.items():
        so_far[at] = so_far.get(at, 0) + times * n


def place(stages, chain):
    return [(at, Item(kind, chain)) for at, kind in stages]


def merged(*placed):
    return [item for _, item in sorted((x for p in placed for x in p), key=lambda x: x[0])]


def make_plans():
    so_far = {}
    plans = {}
    prep = ["F", "X", "L", "P0", "P1", "N1", "N2", "K", "Q0", "Q1"]
    mid = ["O", "W", "F", "X", "P0", "P1", "N1", "N2", "K", "Q0", "Q1"]
    last = ["O", "W", "Z", "X", "H0", "H1", "H2", "H3", "Y"]

    def staggered(kinds, chain, first, apart=1.0):
        return place([(first + apart * n, k) for n, k in enumerate(kinds)], chain)

    chains = [Chain("global", 6 + n, 0, n, "act") for n in range(2)]
    plans["start"] = merged(*(staggered(prep, c, 1.5 * c.half) for c in chains))
    count_up(plans["start"], so_far, 1)

    def global_body(chain, stages):
        steps = [(float(n), Item("att", step=n % STEPS, unit=n // STEPS)) for n in range(2 * STEPS)]
        done = [(u * STEPS + s, u, qc) for u in range(2) for qc, s in enumerate((LAST_QC0, STEPS - 1))]
        outs = [(at + 0.1, Item("evac", unit=u, qc=qc)) for at, u, qc in done]
        toks = [(min(at + 2, 2 * STEPS - 1) + 0.2, Item("tok", unit=u, qc=qc, bank=7)) for at, u, qc in done]
        return merged(steps, outs, toks, place(stages, chain))

    chain = Chain("global", 7, 1, None, "dve")
    plans["A"] = global_body(chain, [(0.5, "F"), (2.5, "X"), (3.5, "L"), (4.5, "P0"), (5.5, "P1"), (6.5, "N1"),
                                     (9.5, "N2"), (12.5, "K"), (14.5, "Q0"), (15.5, "Q1")])
    count_up(plans["A"], so_far, 2)
    chain = Chain("local", 7, 0, None, "dve")
    plans["B"] = global_body(chain, [(-1, "ocur"), (0.5, "O"), (1.5, "W"), (1.6, "F"), (5.5, "X"), (7.5, "P0"),
                                     (8.5, "P1"), (8.6, "N1"), (11.5, "N2"), (14.5, "K"), (16.5, "Q0"),
                                     (17.5, "Q1")])
    count_up(plans["B"], so_far, 2)

    def local_steps(first, places):
        return [(at, Item("local", step=first + n)) for n, at in enumerate(places)]

    chains = [Chain("local", 6 + n, 1, n, "act") for n in range(2)]
    weights = [(14.0, Item("gamma", bank=7)), (15.0, Item("wt1", bank=7)), (15.1, Item("wt2", bank=7))]
    plans["C"] = merged(weights, staggered(mid, chains[0], -0.5), staggered(mid, chains[1], 1.6),
                        local_steps(0, [0.8 + 1.7 * n for n in range(8)]))
    count_up(plans["C"], so_far, 1)
    chains = [Chain("tail", 6 + n, 0, n, "act") for n in range(2)]
    plans["D"] = merged(staggered(last, chains[0], 0), staggered(last, chains[1], 2.6),
                        local_steps(8, [2.8 + 1.3 * n for n in range(8)]))
    count_up(plans["D"], so_far, 1)
    chains = [Chain("tail", 6 + n, 1, n, "act") for n in range(2)]
    plans["end"] = merged(staggered(last, chains[0], 0), staggered(last, chains[1], 1.6))
    count_up(plans["end"], so_far, 1)
    return plans


PLANS = make_plans()

def build(nc, hidden, norm1_w, norm2_w, g_wq, g_kv_down, g_k_up, g_v_up, g_wo,
          l_wq, l_wk, l_wv, l_wo, w1, b1, w2, b2, rope_tab, out):
    F32, BF16, I32 = mybir.dt.float32, mybir.dt.bfloat16, mybir.dt.int32
    ACT, ALU, AX = mybir.ActivationFunctionType, mybir.AluOpType, mybir.AxisListType
    PHASE = {"global": 0, "local": 1}
    ctx = ExitStack()
    with ctx:
        def sb(name, shape, dt=F32):
            return ctx.enter_context(nc.sbuf_tensor(name, shape, dt))

        def sem(name):
            return ctx.enter_context(nc.semaphore(name))

        def per_bank(make):
            return {bank: make(bank) for bank in (6, 7)}

        q_rows = nc.dram_tensor("q_rows", (2, UNITS, ROWS3, GROUP, SEQ), BF16, kind="Internal").ap()
        k_rows = nc.dram_tensor("k_rows", (2, UNITS, ROWS3, SEQ), BF16, kind="Internal").ap()
        x0 = sb("x0", [P, TILES, D])
        x1 = sb("x1", [P, TILES, D])
        heads_out = sb("heads_out", [P, TILES, D])
        v_all = sb("v_all", [P, TILES, KVW])
        v_prev = sb("v_prev", [P, TILES, KVW])
        q_parts = sb("q_parts", [GROUP * ROWS3, UNITS, SEQ], BF16)
        k_parts = sb("k_parts", [KV_HEADS * ROWS3, BATCH, SEQ], BF16)
        ident = sb("ident", [P, P])
        ident_bf = sb("ident_bf", [P, P], BF16)
        ones = sb("ones", [P, P])
        rope = sb("rope", [P, KT, 2, 2 * HD])
        norm_w = [sb("norm_w_global", [P, 1]), sb("norm_w_local", [P, 1])]
        wq_g = sb("wq_g", [P, QW])
        wdown = sb("wdown", [P, LATENT])
        wup = sb("wup", [LATENT, 2 * KVW])
        wqkv_l = sb("wqkv_l", [P, QKW + KVW])
        wo = [sb("wo_g", [P, D]), sb("wo_l", [P, D])]
        w1n, w2n = sb("w1n", [P, FF // P, D]), sb("w2n", [P, FF])
        w1q, w2q = sb("w1q", [P, FF]), sb("w2q", [P, FF // P, D])
        b1c = sb("b1c", [P, FF // P])
        b2b = sb("b2b", [P, D])
        wsum = sb("wsum", [P, 2])
        threshold, minus_threshold = sb("threshold", [P, 2]), sb("minus_threshold", [P, 2])
        o_cur = sb("o_cur", [P, CT, D])
        o_t = per_bank(lambda n: sb(f"o_t{n}", [P, CHUNK]))
        xs = per_bank(lambda n: sb(f"xs{n}", [P, CT, D]))
        xn_t = per_bank(lambda n: sb(f"xn_t{n}", [P, CHUNK]))
        lat_t = per_bank(lambda n: sb(f"lat_t{n}", [LATENT, CHUNK]))
        rot = per_bank(lambda n: sb(f"rot{n}", [P, CT, QKW]))
        parts = per_bank(lambda n: sb(f"parts{n}", [P, CT, QKH, ROWS3], BF16))
        z = per_bank(lambda n: sb(f"z{n}", [P, CT, D]))
        square = sb("square", [P, CT, QKW])
        rot_b = sb("rot_b", [P, CT // 2, QKW])
        rest = sb("rest", [P, CT, QKW])
        sums, inverse = sb("sums", [P, CT * QKH]), sb("inverse", [P, CT * QKH])
        newton_v, newton_t = sb("newton_v", [P, CT * QKH]), sb("newton_t", [P, CT * QKH])
        stats, moments = sb("stats", [P, CT, 6]), sb("moments", [P, CT, 2])
        qs = [sb(f"qs{i}", [P, GROUP, SEQ], BF16) for i in range(2)]
        ks = [sb(f"ks{i}", [P, WIN + SEQ], BF16) for i in range(2)]
        kb = [sb(f"kb{i}", [P, WIN + SEQ], BF16) for i in range(2)]
        wide = sb("wide", [P, RING * PER_STEP, BANK])
        probs = [wide[:, PER_STEP * i:PER_STEP * (i + 1), :] for i in range(RING)]
        probs_l = [wide[:, 2 * i:2 * (i + 1), :] for i in range(2)]
        h_t = {6: wide[:, 4:8, :], 7: wide[:, 8:12, :]}
        vs = [sb(f"vs{i}", [P, KT, 32]) for i in range(2)]
        v_diag = [[sb(f"v_{n}{i}", [P, KT, P]) for i in range(2)] for n in ("own", "before")]
        acc_t = [sb(f"acc_t{i}", [P, BANK]) for i in range(2)]
        sums_inv = sb("sums_inv", [P, CT * GROUP])

        ps = ctx.enter_context(nc.psum_tensor("ps", [P, 8, BANK], F32))
        ACC = 6

        x_in = [sem(f"x_in{c}") for c in range(CHUNKS)]
        prep_in = sem("prep_in")
        rest_in = sem("rest_in")
        consts = sem("consts")
        pool_c = sem("pool_c")
        pool_go = sem("pool_go")
        filled = per_bank(lambda n: sem(f"filled{n}"))
        read = per_bank(lambda n: sem(f"read{n}"))
        xs_ready = per_bank(lambda n: sem(f"xs_ready{n}"))
        parts_ready = per_bank(lambda n: sem(f"parts_ready{n}"))
        o_ready = sem("o_ready")
        result = per_bank(lambda n: sem(f"result{n}"))
        dve_link = per_bank(lambda n: sem(f"dve_link{n}"))
        w_sums, w_ternary = sem("w_sums"), sem("w_ternary")
        scored_g, exped_g, masked_g = sem("scored_g"), sem("exped_g"), sem("masked_g")
        p_free_g = sem("p_free_g")
        stack_free = sem("stack_free")
        evac_g = sem("evac_g")
        v_ready_g = sem("v_ready_g")
        scored_l, exped_l, weighted_l = sem("scored_l"), sem("exped_l"), sem("weighted_l")
        acc_read_l, out_l = sem("acc_read_l"), sem("out_l")
        inv_l = sem("inv_l")
        v_ready_l = sem("v_ready_l")
        parts_out = [[sem(f"parts_out_{ph}{b}") for b in range(BATCH)] for ph in ("global", "local")]
        stack_in = [[sem(f"stack_in{u}_{part}") for part in ("first", "second", "all")] for u in range(2)]
        v_shifted = [sem(f"v_shifted{b}") for b in range(BATCH)]
        stored = sem("stored")

        block = ctx.enter_context(nc.Block())

        LOOPS = {"A": (0, 0), "B": (KV_HEADS, 1)}

        def value(counts, it=0):
            before, per, within = counts
            return it * per + (before + within) if per else before + within

        def tiles(chain, it, first=0, n=CT):
            at = chain.batch * KT + first
            if chain.half is None:
                return bass.ds(it * CT + at, n)
            return slice(at + chain.half * CT, at + chain.half * CT + n)

        def tokens(chain, it):
            return bass.ds(it * CHUNK, CHUNK) if chain.half is None else slice(chain.half * CHUNK, (chain.half + 1) * CHUNK)

        def bank_bf(bank):
            return ps[:, bank, :].bitcast(BF16)

        HALF_DMAS = 2 * PARTS
        LOCAL_DMAS = 1 + 2 * PARTS
        OUT_DMAS = 1 + KV_HEADS

        @block.sync
        def _(sp):
            src = hidden.rearrange("b (t p) d -> p (b t) d", p=P)

            def load_x(c):
                sp.dma_start(x0[:, c * CT:(c + 1) * CT, :], src[:, c * CT:(c + 1) * CT, :]).then_inc(x_in[c], 16)

            load_x(0)
            sp.dma_start(norm_w[0][:, :], norm1_w.rearrange("(p a) -> p a", a=1)).then_inc(prep_in, 16)
            sp.dma_start(wdown[:, :], g_kv_down).then_inc(prep_in, 16)
            sp.dma_start(wup[:, 0:KVW], g_k_up).then_inc(prep_in, 16)
            sp.dma_start(wup[:, KVW:2 * KVW], g_v_up).then_inc(prep_in, 16)
            sp.dma_start(wq_g[:, :], g_wq).then_inc(prep_in, 16)
            sp.dma_start(rope[:, :, :, :], rope_tab.rearrange("(t p) h c -> p t h c", p=P)).then_inc(prep_in, 16)
            for c in range(1, CHUNKS):
                load_x(c)
            for dst, s in ((norm_w[1][:, :], norm2_w.rearrange("(p a) -> p a", a=1)),
                           (wo[0][:, :], g_wo), (wo[1][:, :], l_wo), (wqkv_l[:, 0:QW], l_wq),
                           (wqkv_l[:, QW:QKW], l_wk), (wqkv_l[:, QKW:QKW + KVW], l_wv),
                           (b2b[:, :], b2.partition_broadcast(P)),
                           (w1n[:, :, :], w1.rearrange("(a p) d -> p a d", p=P)), (w2n[:, :], w2)):
                sp.dma_start(dst, s).then_inc(rest_in, 16)
            sp.dma_start(b1c[:, :], b1.rearrange("(a p) -> p a", p=P), allow_slow_non_contiguous=True)\
                .then_inc(rest_in, 16)

            stores = {(phase, b): 0 for phase in range(2) for b in range(BATCH)}

            def store(chain, stage, it=0):
                phase, b = PHASE[chain.what], chain.batch
                half = it if chain.half is None else chain.half
                tok = slice(half * CHUNK, (half + 1) * CHUNK)
                unit = b * KV_HEADS
                sp.wait_ge(read[chain.bank], value(chain.items[stage].counts["use"], it))
                if stage == "K":
                    sp.dma_start(k_rows[phase, unit:unit + KV_HEADS, :, tok].rearrange("u r n -> (u r) n"),
                                 k_parts[:, b, tok]).then_inc(parts_out[phase][b], 16)
                    stores[phase, b] += 1
                else:
                    for g in range(unit + 2 * int(stage[1]), unit + 2 * int(stage[1]) + 2):
                        sp.dma_start(q_rows[phase, g, :, :, tok].rearrange("r h n -> h r n"), q_parts[:, g, tok])\
                            .then_inc(parts_out[phase][b], 16)
                        stores[phase, b] += 1

            def store_all(chain, it=0):
                for stage in ("K", "Q0", "Q1"):
                    store(chain, stage, it)

            def load_stacks(phase, unit, first=0, n=SEQ):
                u, batch = unit % 2, unit // KV_HEADS
                landed = stack_in[u][2 if n == SEQ else first // CHUNK]
                sp.wait_ge(parts_out[phase][batch], stores[phase, batch] * 16)
                sp.wait_ge(stack_free, phase * UNITS + unit + 1)
                for dst in (ks, kb)[:phase + 1]:
                    for j in range(PARTS):
                        sp.dma_start(dst[u][j * ROWS3:(j + 1) * ROWS3, WIN + first:WIN + first + n],
                                     k_rows[phase, unit, j * HD:(j + 1) * HD, first:first + n].unsqueeze(0)
                                     .broadcast_to([PARTS, HD, n])).then_inc(landed, 16)
                if n == SEQ:
                    sp.dma_start(qs[u][0:STACK, :, :].rearrange("p h n -> p (h n)"),
                                 q_rows[phase, unit].rearrange("r h n -> r (h n)").unsqueeze(0)
                                 .broadcast_to([PARTS, ROWS3, GROUP * SEQ])).then_inc(landed, 16)
                else:
                    for j in range(PARTS):
                        sp.dma_start(qs[u][j * ROWS3:(j + 1) * ROWS3, :, first:first + n],
                                     q_rows[phase, unit, :, :, first:first + n]).then_inc(landed, 16)

            def shift_v(b, chains, times):
                for chain in chains:
                    sp.wait_ge(read[chain.bank], value(chain.items["P1"].counts["use"], times - 1))
                ts = slice(b * KT, (b + 1) * KT)
                sp.dma_start(v_prev[WIN:P, ts, :], v_all[0:P - WIN, ts, :]).then_inc(v_shifted[b], 16)
                sp.dma_start(v_prev[0:WIN, b * KT + 1:(b + 1) * KT, :],
                             v_all[P - WIN:P, b * KT:(b + 1) * KT - 1, :]).then_inc(v_shifted[b], 16)

            def chains_of(name):
                return sorted({i.chain for i in PLANS[name] if i.chain}, key=lambda c: c.half or 0)

            def load_global(*units):
                for unit in units:
                    for first in (0, CHUNK):
                        load_stacks(0, unit, first, CHUNK)

            def load_local(*units):
                for unit in units:
                    load_stacks(1, unit)

            sp.wait_ge(consts, 2)
            c0, c1 = chains_of("start")
            store(c0, "K")
            store(c0, "Q0")
            load_stacks(0, 0, 0, CHUNK)
            store(c1, "K")
            store(c1, "Q0")
            load_stacks(0, 0, CHUNK, CHUNK)
            load_global(1)
            store(c0, "Q1")
            store(c1, "Q1")
            load_global(2)
            store_all(chains_of("A")[0], 0)
            load_global(3)
            store_all(chains_of("A")[0], 1)
            load_global(4, 5, 6)
            store_all(chains_of("B")[0], 0)
            load_global(7)
            store_all(chains_of("B")[0], 1)
            shift_v(0, chains_of("B"), 2)
            load_local(0, 1, 2, 3)
            for chain in chains_of("C"):
                store_all(chain)
            shift_v(1, chains_of("C"), 1)
            load_local(4, 5, 6, 7)
            dst = out.rearrange("b (t p) d -> p (b t) d", p=P)
            n = 0
            for name in ("D", "end"):
                for chain in chains_of(name):
                    sp.wait_ge(result[chain.bank], value(chain.items["Y"].counts["y"]))
                    sp.dma_start(dst[:, tiles(chain, 0), :], x1[:, tiles(chain, 0), :]).then_inc(stored, 16)
                    n += 16
            sp.wait_ge(stored, n)

        @block.gpsimd
        def _(pool):
            chained = [0]

            def link(ins):
                chained[0] += 1
                ins.then_inc(pool_c, 1)
                pool.wait_ge(pool_c, chained[0])

            nc.gpsimd.memset(ones[:, :], 1.0)
            nc.gpsimd.memset(ident[:, :], 0.0)
            link(nc.gpsimd.memset(ident_bf[:, :], 0.0))
            for m in (ident, ident_bf):
                last = nc.gpsimd.affine_select(out=m[:, :], in_=m[:, :], compare_op=ALU.not_equal, fill=1.0,
                                               base=0, pattern=[[-1, P]], channel_multiplier=1)
            last.then_inc(consts, 1)

            def local_constants():
                for i in range(2):
                    nc.gpsimd.memset(vs[i][:, :, :], 1.0)
                    nc.gpsimd.memset(ks[i][:, :], 0.0)
                    nc.gpsimd.memset(kb[i][:, :], 0.0)
                    for n in range(2):
                        nc.gpsimd.memset(v_diag[n][i][:, :, :], 0.0)
                link(nc.gpsimd.memset(v_prev[:, :, :], 0.0))
                for i in range(2):
                    ins = nc.gpsimd.memset(qs[i][2 * WIN:P, :, :], 0.0)
                link(ins)
                rows = slice(P - WIN, P)
                for i in range(2):
                    place = qs[i][rows, :, :].rearrange("p h (b q) -> p (h b) q", q=WIN)
                    nc.gpsimd.affine_select(out=place, in_=place, compare_op=ALU.not_equal, fill=1.0, base=0,
                                            pattern=[[0, GROUP * SEQ // WIN], [1, WIN]], channel_multiplier=-1)
                    own = ks[i][rows, :].rearrange("p (b k) -> p b k", k=WIN)
                    nc.gpsimd.affine_select(out=own, in_=own, compare_op=ALU.is_ge, fill=MASKED, base=0,
                                            pattern=[[0, 1 + SEQ // WIN], [-1, WIN]], channel_multiplier=1)
                    old = kb[i][rows, :].rearrange("p (b k) -> p b k", k=WIN)
                    nc.gpsimd.affine_select(out=old, in_=old, compare_op=ALU.is_gt, fill=MASKED, base=0,
                                            pattern=[[0, 1 + SEQ // WIN], [1, WIN]], channel_multiplier=-1)
                for j in range(P // WIN):
                    rows = slice(j * WIN, (j + 1) * WIN)
                    for i in range(2):
                        for n in range(2):
                            first = 1 if (n, j) == (1, 0) else 0
                            last = nc.gpsimd.memset(v_diag[n][i][rows, first:, j * WIN + HD:(j + 1) * WIN], 1.0)
                last.then_inc(consts, 1)
                pool.wait_ge(consts, 2)

            def current_outputs(item, it):
                nc.gpsimd.tensor_copy(o_cur[:, :, :], heads_out[:, tiles(item.chain, it), :]).then_inc(o_ready, 1)

            def mask(unit, s):
                pool.wait_ge(exped_g, unit * STEPS + s + 1)
                pool.sem_inc(pool_go, 1)
                for first, n, cols in diagonal_runs(s):
                    for at in cols:
                        blk = probs[s % RING][:, first:first + n, at:at + P]
                        last = nc.gpsimd.affine_select(out=blk, in_=blk, compare_op=ALU.is_ge, fill=0.0, base=0,
                                                       pattern=[[0, n], [1, P]], channel_multiplier=-1)
                last.then_inc(masked_g, 1)

            local_constants()
            for name, (before, batch) in LOOPS.items():
                if name == "B":
                    pool.wait_ge(read[7], value(PLANS["A"][-1].counts["use"], 1))
                with pool.Fori(0, 2) as it:
                    for item in PLANS[name]:
                        if item.kind == "att":
                            unit = it * 2 + (before + item.unit)
                            if item.step == 0:
                                pool.wait_ge(evac_g, unit * 2 + 1)
                                src = v_all[:, batch * KT:(batch + 1) * KT, bass.ds((it * 2 + item.unit) * HD, HD)]
                                nc.gpsimd.tensor_copy(vs[item.unit][:, :, 0:HD], src).then_inc(v_ready_g, 1)
                            if item.step in MASKED_STEPS:
                                mask(unit, item.step)
                        elif item.kind == "ocur":
                            current_outputs(item, it)

            def build_v_diag(unit):
                b, g = unit // KV_HEADS, unit % KV_HEADS
                if unit >= 2:
                    pool.wait_ge(weighted_l, LOCAL_STEPS * (unit - 1))
                if g == 0:
                    pool.wait_ge(v_shifted[b], 32)
                for n, v in ((0, v_all), (1, v_prev)):
                    for j in range(P // WIN):
                        rows = slice(j * WIN, (j + 1) * WIN)
                        last = nc.gpsimd.tensor_copy(v_diag[n][unit % 2][rows, :, j * WIN:j * WIN + HD],
                                                     v[rows, b * KT:(b + 1) * KT, g * HD:(g + 1) * HD])
                last.then_inc(v_ready_l, 1)
                pool.wait_ge(v_ready_l, unit + 1)

            pool.wait_ge(masked_g, UNITS * len(MASKED_STEPS))
            for name in ("C", "D"):
                for item in PLANS[name]:
                    if item.kind == "local":
                        unit, step = divmod(item.step, LOCAL_STEPS)
                        if step == 0 and unit % KV_HEADS == 0:
                            build_v_diag(unit)
                        if step == 0 and unit % KV_HEADS < KV_HEADS - 1:
                            build_v_diag(unit + 1)

        @block.scalar
        def _(act):
            def copy(item, dst, src, **more):
                n = item.bank
                act.wait_ge(filled[n], value(item.counts["use"]))
                nc.scalar.activation(dst, src, more.pop("func", ACT.Copy), **more).then_inc(read[n], 1)

            def side(item):
                c = item.chain
                if c is None or c.copies != "act":
                    return
                n, kind = c.bank, item.kind
                if kind == "O":
                    copy(item, o_t[n][:, :], ps[:, n, :])
                elif kind == "X" and c.what == "tail":
                    copy(item, xn_t[n][:, :], ps[:, n, :])
                elif kind == "X":
                    copy(item, xn_t[n][:, :], ps[:, n, :], scale=norm_w[PHASE[c.what]][:, :])
                elif kind == "L":
                    copy(item, lat_t[n][:, :], ps[0:LATENT, n, :])
                elif kind in ("Q0", "Q1"):
                    g = c.batch * KV_HEADS + 2 * int(kind[1])
                    copy(item, q_parts[:, g:g + 2, tokens(c, 0)],
                         bank_bf(n)[0:GROUP * ROWS3, :].rearrange("p (g n) -> p g n", g=2))
                elif kind in ("H0", "H1", "H2", "H3"):
                    f = int(kind[1])
                    copy(item, h_t[n][:, f, :], ps[:, n, :], func=ACT.Relu, bias=b1c[:, f:f + 1])

            act.wait_ge(prep_in, 6 * 16)
            for item in PLANS["start"]:
                side(item)
            for name, (before, _) in LOOPS.items():
                with act.Fori(0, 2) as it:
                    for item in PLANS[name]:
                        if item.kind == "att":
                            step = (it * 2 + (before + item.unit)) * STEPS + item.step
                            act.wait_ge(scored_g, step + 1)
                            act.wait_ge(p_free_g, step + 1)
                            slot = (item.step % 2) * PER_STEP
                            nc.scalar.activation(probs[item.step % RING][:, :, :], ps[:, slot:slot + PER_STEP, :],
                                                 ACT.Exp, scale=SCALE).then_inc(exped_g, 1)
            act.wait_ge(rest_in, 10 * 16)
            act.wait_ge(parts_out[0][1], 2 * OUT_DMAS * 16)
            for name in ("C", "D", "end"):
                for item in PLANS[name]:
                    if item.kind == "local":
                        s = item.step % LOCAL_STEPS
                        act.wait_ge(scored_l, item.step + 1)
                        if item.step >= 2:
                            act.wait_ge(weighted_l, item.step - 1)
                        nc.scalar.activation(probs_l[s][:, :, :], ps[:, 2 * s:2 * s + 2, :], ACT.Exp, scale=SCALE)\
                            .then_inc(exped_l, 1)
                    else:
                        side(item)

        @block.vector
        def _(dve):
            def linker(item, it):
                sem_, total = dve_link[item.bank], ADDS[item.kind]["link"]
                start, n = value(item.counts["link"], it) - total, [0]

                def link(ins):
                    n[0] += 1
                    ins.then_inc(sem_, 1)
                    dve.wait_ge(sem_, start + n[0])

                def done():
                    assert n[0] == total, (item.kind, n[0])
                return link, done

            def inverse_root(link, y, total, scale, eps):
                n = y.shape[1]
                v, t = newton_v[:, 0:n], newton_t[:, 0:n]
                link(nc.vector.tensor_scalar(v, total, scale, eps, ALU.mult, ALU.add))
                link(nc.vector.tensor_scalar(t.bitcast(I32), v.bitcast(I32), 1, None, ALU.logical_shift_right))
                link(nc.vector.tensor_scalar(y.bitcast(I32), t.bitcast(I32), -1.0, float(0x5F3759DF), ALU.mult, ALU.add))
                for _ in range(3):
                    link(nc.vector.tensor_tensor(t, y, y, ALU.mult))
                    link(nc.vector.scalar_tensor_tensor(out=t, in0=t, scalar=-0.5, in1=v, op0=ALU.mult, op1=ALU.mult))
                    link(nc.vector.scalar_tensor_tensor(out=y, in0=t, scalar=1.5, in1=y, op0=ALU.add, op1=ALU.mult))

            def of_heads(x):
                return x.rearrange("p t (h d) -> p (t h) d", d=HD)

            def wide_bank(n):
                return ps[:, n, :].rearrange("p (t d) -> p t d", d=D)

            def filled_by_pe(item, it):
                dve.wait_ge(filled[item.bank], value(item.counts["use"], it))

            def copy(item, it, dst, src):
                filled_by_pe(item, it)
                nc.vector.tensor_copy(dst, src).then_inc(read[item.bank], 1)

            def side(item, it=0):
                c, n, kind = item.chain, item.bank, item.kind
                ph = PHASE.get(c.what)
                if kind == "O" and c.copies == "dve":
                    copy(item, it, o_t[n][:, :], ps[:, n, :])
                elif kind == "X" and c.copies == "dve":
                    filled_by_pe(item, it)
                    nc.vector.tensor_scalar(xn_t[n][:, :], ps[:, n, :], norm_w[ph][:, :], None, ALU.mult)\
                        .then_inc(read[n], 1)
                elif kind == "L" and c.copies == "dve":
                    copy(item, it, lat_t[n][:, :], ps[0:LATENT, n, :])
                elif kind in ("Q0", "Q1") and c.copies == "dve":
                    g = c.batch * KV_HEADS + 2 * int(kind[1])
                    copy(item, it, q_parts[:, g:g + 2, tokens(c, it)],
                         bank_bf(n)[0:GROUP * ROWS3, :].rearrange("p (g n) -> p g n", g=2))
                elif kind == "K":
                    copy(item, it, k_parts[:, c.batch, tokens(c, it)], bank_bf(n)[0:KV_HEADS * ROWS3, 0:CHUNK])
                elif kind == "W":
                    filled_by_pe(item, it)
                    if c.what == "tail":
                        before = value(c.items["Y"].counts["y"]) - 1
                        if before:
                            dve.wait_ge(result[n], before)
                        nc.vector.tensor_tensor(z[n][:, :, :], x1[:, tiles(c, it), :], wide_bank(n), ALU.add)\
                            .then_inc(read[n], 1)
                    else:
                        nc.vector.tensor_tensor(x1[:, tiles(c, it), :], x0[:, tiles(c, it), :], wide_bank(n), ALU.add)\
                            .then_inc(read[n], 1)
                elif kind == "F":
                    link, done = linker(item, it)
                    if c.what == "local":
                        dve.wait_ge(read[n], value(c.items["W"].counts["use"], it))
                        x = x1[:, tiles(c, it), :]
                    else:
                        x = x0[:, tiles(c, it), :]
                        if c.half is not None:
                            dve.wait_ge(x_in[c.half], 16)
                    link(nc.vector.tensor_tensor(square[:, :, 0:D], x, x, ALU.mult))
                    link(nc.vector.reduce_sum(sums[:, 0:CT], square[:, :, 0:D], AX.X))
                    inverse_root(link, inverse[:, 0:CT], sums[:, 0:CT], 1.0 / D, EPS_RMS)
                    nc.vector.tensor_tensor(xs[n][:, :, :], x, inverse[:, 0:CT].unsqueeze(2)
                                            .broadcast_to([P, CT, D]), ALU.mult).then_inc(xs_ready[n], 1)
                    done()
                elif kind in ("P0", "P1"):
                    link, done = linker(item, it)
                    t0 = (CT // 2) * int(kind[1])
                    pj = ps[:, n, :].rearrange("p (t f) -> p t f", f=BANK // 2)
                    filled_by_pe(item, it)
                    nc.vector.tensor_copy(v_all[:, tiles(c, it, t0, CT // 2), :], pj[:, :, QKW:QKW + KVW])
                    at = bass.ds(it * CT + t0, CT // 2) if c.half is None else slice(c.half * CT + t0, c.half * CT + t0 + CT // 2)
                    half_rot = rot[n][:, t0:t0 + CT // 2, :]
                    nc.vector.tensor_tensor(half_rot.rearrange("p t (h d) -> p t h d", d=HD),
                                            pj[:, :, 0:QKW].rearrange("p t (h d) -> p t h d", d=HD),
                                            rope[:, at, ph, 0:HD].unsqueeze(2).broadcast_to([P, CT // 2, QKH, HD]),
                                            ALU.mult)
                    pairs = "p t (h e o) -> p t h e o"
                    for odd in range(2):
                        sin = rope[:, at, ph, HD + odd * HD // 2:HD + (odd + 1) * HD // 2]
                        ins = nc.vector.tensor_tensor(
                            rot_b[:, :, :].rearrange(pairs, e=HD // 2, o=2)[:, :, :, :, odd],
                            pj[:, :, 0:QKW].rearrange(pairs, e=HD // 2, o=2)[:, :, :, :, 1 - odd],
                            sin.unsqueeze(2).broadcast_to([P, CT // 2, QKH, HD // 2]), ALU.mult)
                    ins.then_inc(read[n], 1)
                    dve.wait_ge(read[n], value(item.counts["use"], it))
                    link(nc.vector.tensor_tensor(half_rot, half_rot, rot_b[:, :, :], ALU.add))
                    done()
                elif kind == "N1":
                    link, done = linker(item, it)
                    link(nc.vector.tensor_tensor(square[:, :, :], rot[n][:, :, :], rot[n][:, :, :], ALU.mult))
                    link(nc.vector.reduce_sum(sums[:, :], of_heads(square[:, :, :]), AX.X))
                    inverse_root(link, inverse[:, :], sums[:, :], 1.0 / HD, EPS_RMS)
                    link(nc.vector.tensor_tensor(of_heads(rot[n][:, :, :]), of_heads(rot[n][:, :, :]), inverse[:, :]
                                                 .unsqueeze(2).broadcast_to([P, CT * QKH, HD]), ALU.mult))
                    done()
                elif kind == "N2":
                    link, done = linker(item, it)
                    part = [parts[n][:, :, :, i * HD:(i + 1) * HD].rearrange("p t h d -> p (t h) d") for i in range(PARTS)]
                    full, left = of_heads(rot[n][:, :, :]), of_heads(rest[:, :, :])
                    link(nc.vector.tensor_copy(part[0], full))
                    link(nc.vector.tensor_tensor(left, full, part[0], ALU.subtract))
                    link(nc.vector.tensor_copy(part[1], left))
                    nc.vector.tensor_tensor(part[2], left, part[1], ALU.subtract).then_inc(parts_ready[n], 1)
                    done()
                elif kind in ("Z", "Y"):
                    link, done = linker(item, it)
                    y = z[n]
                    if kind == "Z":
                        dve.wait_ge(read[n], value(c.items["W"].counts["use"]))
                        link(nc.vector.tensor_tensor(y[:, :, :], y[:, :, :], x0[:, tiles(c, 0), :], ALU.add))
                    else:
                        filled_by_pe(item, 0)
                        nc.vector.tensor_tensor(y[:, :, :], wide_bank(n),
                                                b2b[:, :].unsqueeze(1).broadcast_to([P, CT, D]), ALU.add)\
                            .then_inc(read[n], 1)
                        dve.wait_ge(read[n], value(item.counts["use"]))
                        link(nc.vector.tensor_tensor(y[:, :, :], y[:, :, :], xs[n][:, :, :], ALU.add))
                    for t in range(CT):
                        ins = nc.vector.bn_stats(stats[:, t, :], y[:, t, :])
                    link(ins)
                    for t in range(CT):
                        ins = nc.vector.bn_aggr(moments[:, t, :], stats[:, t, :])
                    link(ins)
                    inverse_root(link, inverse[:, 0:CT], moments[:, :, 1], 1.0, EPS_LN)
                    first = tiles(c, 0).start
                    for t in range(CT):
                        to = xs[n][:, t, :] if kind == "Z" else x1[:, first + t, :]
                        ins = nc.vector.tensor_scalar(to, y[:, t, :], moments[:, t, 0:1], inverse[:, t:t + 1],
                                                      ALU.subtract, ALU.mult)
                    ins.then_inc(xs_ready[n] if kind == "Z" else result[n], 1)
                    done()

            def normalised(o, dst, link):
                inv = sums_inv[:, :].rearrange("p (t h) -> p t h", h=GROUP)
                link(nc.vector.reciprocal(inv, o[:, :, :, HD]))
                return nc.vector.tensor_tensor(dst.rearrange("p t (h d) -> p t h d", d=HD), o[:, :, :, 0:HD],
                                               inv.unsqueeze(3).broadcast_to([P, CT, GROUP, HD]), ALU.mult)

            def ternary_weights(item):
                link, done = linker(item, 0)
                views = [w1n[:, :, :].rearrange("p a d -> p (a d)"), w2n[:, :]]
                tmp = [rest[:, :, :].rearrange("p a d -> p (a d)")[:, 0:FF], square[:, :, :].rearrange("p a d -> p (a d)")[:, 0:FF]]
                for i in range(2):
                    ins = nc.vector.scalar_tensor_tensor(out=tmp[i], in0=views[i], scalar=-1.0, in1=views[i],
                                                         op0=ALU.mult, op1=ALU.max)
                link(ins)
                for i in range(2):
                    ins = nc.vector.reduce_sum(wsum[:, i:i + 1], tmp[i], AX.X)
                ins.then_inc(w_sums, 1)
                filled_by_pe(item, 0)
                nc.vector.tensor_scalar(threshold[:, :], ps[:, item.bank, 0:2], 1.0 / (FF * D), EPS_Q, ALU.mult, ALU.add)\
                    .then_inc(read[item.bank], 1)
                dve.wait_ge(read[item.bank], value(item.counts["use"]))
                link(nc.vector.tensor_scalar(threshold[:, :], threshold[:, :], 0.5, None, ALU.mult))
                link(nc.vector.tensor_scalar(minus_threshold[:, :], threshold[:, :], -1.0, None, ALU.mult))
                for i in range(2):
                    link(nc.vector.tensor_scalar(tmp[i], views[i], minus_threshold[:, i:i + 1], None, ALU.is_lt))
                    ins = nc.vector.scalar_tensor_tensor(out=views[i], in0=views[i], scalar=threshold[:, i:i + 1],
                                                         in1=tmp[i], op0=ALU.is_gt, op1=ALU.subtract)
                ins.then_inc(w_ternary, 1)
                done()

            dve.wait_ge(prep_in, 6 * 16)
            for item in PLANS["start"]:
                side(item)
            for c in range(CHUNKS):
                dve.wait_ge(x_in[c], 16)
            dve.sem_inc(evac_g, 3)
            for name, (before, batch) in LOOPS.items():
                if name == "B":
                    dve.wait_ge(parts_out[0][0], 2 * OUT_DMAS * 16)
                with dve.Fori(0, 2) as it:
                    for item in PLANS[name]:
                        if item.kind == "evac":
                            unit = it * 2 + (before + item.unit)
                            freed = sum(FREED[s] for s in range(STEPS) if item.qc or s <= LAST_QC0)
                            dve.wait_ge(p_free_g, unit * STEPS + (RING + freed))
                            nc.vector.tensor_copy(acc_t[item.qc][:, :], ps[:, ACC, :]).then_inc(evac_g, 1)
                        elif item.kind == "tok":
                            link, done = linker(item, it)
                            filled_by_pe(item, it)
                            o = ps[:, item.bank, :].rearrange("p (t h c) -> p t h c", t=CT, c=32)
                            dst = heads_out[:, batch * KT + item.qc * CT:batch * KT + (item.qc + 1) * CT,
                                            bass.ds((it * 2 + item.unit) * GROUP * HD, GROUP * HD)]
                            normalised(o, dst, link).then_inc(read[item.bank], 1)
                            done()
                        elif item.chain:
                            side(item, it)
            dve.wait_ge(parts_out[0][1], 2 * OUT_DMAS * 16)
            for name in ("C", "D", "end"):
                for item in PLANS[name]:
                    if item.kind == "local":
                        unit, s = divmod(item.step, LOCAL_STEPS)
                        b, g = divmod(unit, KV_HEADS)
                        dve.wait_ge(weighted_l, item.step + 1)
                        nc.vector.transpose(acc_t[s][:, :], ps[:, 4 + s, :]).then_inc(acc_read_l, 1)
                        dve.wait_ge(acc_read_l, item.step + 1)

                        def link(ins):
                            ins.then_inc(inv_l, 1)
                            dve.wait_ge(inv_l, item.step + 1)
                        dst = heads_out[:, b * KT + s * CT:b * KT + (s + 1) * CT, g * GROUP * HD:(g + 1) * GROUP * HD]
                        normalised(acc_t[s][:, :].rearrange("p (t h c) -> p t h c", t=CT, c=32), dst, link)\
                            .then_inc(out_l, 1)
                    elif item.kind == "gamma":
                        dve.wait_ge(rest_in, 10 * 16)
                        ternary_weights(item)
                    elif item.kind in ("wt1", "wt2"):
                        to = w1q[:, :] if item.kind == "wt1" else w2q[:, :, :].rearrange("p a d -> p (a d)")
                        copy(item, 0, to, ps[:, item.bank, :])
                    elif item.chain:
                        side(item)

        @block.tensor
        def _(pe):
            def bank_free(item, it):
                before = value(item.counts["use"], it) - 1
                if not isinstance(before, int) or before > 0:
                    pe.wait_ge(read[item.bank], before)

            def transposes(bank, src):
                for t in range(CT):
                    ins = nc.tensor.transpose(ps[:, bank, t * P:(t + 1) * P], src(t), ident[:, :])
                return ins

            def side(item, it=0):
                c, n, kind = item.chain, item.bank, item.kind
                if "use" not in item.counts:
                    return
                bank_free(item, it)
                if kind == "O":
                    if c.half is None:
                        pe.wait_ge(o_ready, value(c.items["ocur"].counts["ocur"], it))
                        ins = transposes(n, lambda t: o_cur[:, t, :])
                    else:
                        if c.what == "tail":
                            pe.wait_ge(out_l, (c.batch + 1) * KV_HEADS * LOCAL_STEPS)
                        ins = transposes(n, lambda t: heads_out[:, tiles(c, 0, t, 1), :].rearrange("p a d -> p (a d)"))
                elif kind == "W":
                    for t in range(CT):
                        ins = nc.tensor.matmul(ps[:, n, t * P:(t + 1) * P], o_t[n][:, t * P:(t + 1) * P],
                                               wo[int(c.what == "tail")][:, :], start=True, stop=True)
                elif kind == "X":
                    pe.wait_ge(xs_ready[n], value(c.items["Z" if c.what == "tail" else "F"].counts["xs"], it))
                    ins = transposes(n, lambda t: xs[n][:, t, :])
                elif kind == "L":
                    ins = nc.tensor.matmul(ps[0:LATENT, n, :], wdown[:, :], xn_t[n][:, :], start=True, stop=True)
                elif kind in ("P0", "P1"):
                    for t in range(CT // 2):
                        tok = slice((t + CT // 2 * int(kind[1])) * P, (t + 1 + CT // 2 * int(kind[1])) * P)
                        to = ps[:, n, t * BANK // 2:t * BANK // 2 + QKW + KVW]
                        if c.what == "global":
                            nc.tensor.matmul(to[:, 0:QW], xn_t[n][:, tok], wq_g[:, :], start=True, stop=True)
                            ins = nc.tensor.matmul(to[:, QW:QKW + KVW], lat_t[n][:, tok], wup[:, :], start=True, stop=True)
                        else:
                            ins = nc.tensor.matmul(to, xn_t[n][:, tok], wqkv_l[:, :], start=True, stop=True)
                elif kind in ("K", "Q0", "Q1"):
                    if kind == "K":
                        pe.wait_ge(parts_ready[n], value(c.items["N2"].counts["parts"], it))
                    for g, first in enumerate([HEADS] if kind == "K" else [2 * int(kind[1]) * GROUP, (2 * int(kind[1]) + 1) * GROUP]):
                        for t in range(CT):
                            src = parts[n][:, t, first:first + GROUP, :].rearrange("p h r -> p (h r)")
                            ins = nc.tensor.transpose(bank_bf(n)[0:GROUP * ROWS3, g * CHUNK + t * P:g * CHUNK + (t + 1) * P],
                                                      src, ident_bf[:, :])
                elif kind[0] == "H":
                    f = int(kind[1])
                    ins = nc.tensor.matmul(ps[:, n, :], w1q[:, f * P:(f + 1) * P], xn_t[n][:, :], start=True, stop=True)
                elif kind == "Y":
                    for t in range(CT):
                        for f in range(FF // P):
                            ins = nc.tensor.matmul(ps[:, n, t * P:(t + 1) * P], h_t[n][:, f, t * P:(t + 1) * P],
                                                   w2q[:, f, :], start=f == 0, stop=f == FF // P - 1)
                elif kind == "gamma":
                    pe.wait_ge(w_sums, 1)
                    ins = nc.tensor.matmul(ps[:, n, 0:2], ones[:, :], wsum[:, :], start=True, stop=True)
                elif kind == "wt1":
                    pe.wait_ge(w_ternary, 1)
                    ins = transposes(n, lambda t: w1n[:, t, :])
                elif kind == "wt2":
                    ins = transposes(n, lambda t: w2n[:, t * P:(t + 1) * P])
                elif kind == "tok":
                    pe.wait_ge(evac_g, item.out_unit * 2 + (item.qc + 4))
                    ins = transposes(n, lambda t: acc_t[item.qc][:, t * P:(t + 1) * P])
                ins.then_inc(filled[n], 1)

            def scores(u, s, pairs):
                if s == 0:
                    pe.wait_ge(stack_in[u][0], pairs * (16 * HALF_DMAS))
                elif s == FILLS_QC0 // PER_STEP:
                    pe.wait_ge(stack_in[u][1], pairs * (16 * HALF_DMAS))
                for n in range(PER_STEP):
                    at = 0
                    for h, kt, q0, w in FILLS[PER_STEP * s + n]:
                        ins = nc.tensor.matmul(ps[:, (s % 2) * PER_STEP + n, at:at + w],
                                               ks[u][0:STACK, WIN + kt * P:WIN + (kt + 1) * P], qs[u][0:STACK, h, q0:q0 + w],
                                               start=True, stop=True)
                        at += w
                ins.then_inc(scored_g, 1)

            def weighted(u, s, unit):
                for n, (qc, pieces) in enumerate(GROUPS.get(s, [])):
                    if n == 0:
                        if s == min(GROUPS):
                            pe.wait_ge(v_ready_g, unit + 1)
                    last = max(fill for _, _, _, _, fill, _ in pieces) // PER_STEP
                    if last == s:
                        pe.wait_ge(exped_g, unit * STEPS + s + 1)
                    masked = sum(m <= last for m in MASKED_STEPS)
                    if masked:
                        pe.wait_ge(masked_g, unit * len(MASKED_STEPS) + masked)
                    kt = pieces[0][1]
                    if kt == 0:
                        pe.wait_ge(evac_g, unit * 2 + (qc + 3))
                    for h, kt, q0, w, fill, at in pieces:
                        to = q0 - qc * CHUNK
                        ins = nc.tensor.matmul(ps[32 * h:32 * h + 32, ACC, to:to + w], vs[u][:, kt, :],
                                               probs[(fill // PER_STEP) % RING][:, fill % PER_STEP, at:at + w],
                                               start=kt == 0, stop=kt == (qc + 1) * CT - 2)
                        if s == STEPS - 3 and n == 0 and h == 0:
                            ins.then_inc(stack_free, 1)
                if FREED[s]:
                    ins.then_inc(p_free_g, FREED[s])

            pe.wait_ge(consts, 1)
            pe.wait_ge(prep_in, 6 * 16)
            pe.sem_inc(stack_free, 2)
            pe.sem_inc(p_free_g, RING)
            for item in PLANS["start"]:
                side(item)
            for s in range(2):
                scores(0, s, 1)
            for name, (before, _) in LOOPS.items():
                if name == "B":
                    pe.wait_ge(rest_in, 10 * 16)
                with pe.Fori(0, 2) as it:
                    for item in PLANS[name]:
                        if item.kind == "att":
                            u, s = item.unit, item.step
                            unit = it * 2 + (before + u)
                            pairs = it + (before // 2 + 1)
                            pe.wait_ge(exped_g, unit * STEPS + s + 1)
                            if s + 2 < STEPS:
                                scores(u, s + 2, pairs)
                            elif u == 0:
                                scores(1, s + 2 - STEPS, pairs)
                            elif name == "A":
                                scores(0, s + 2 - STEPS, pairs + 1)
                            else:
                                with pe.If(it < 1):
                                    scores(0, s + 2 - STEPS, pairs + 1)
                            weighted(u, s, unit)
                        else:
                            if item.kind == "tok":
                                item.out_unit = it * 2 + (before + item.unit)
                            side(item, it)

            def local_scores(step):
                unit, s = divmod(step, LOCAL_STEPS)
                u = unit % 2
                if step >= 2:
                    pe.wait_ge(exped_l, step - 1)
                if s == 0:
                    pe.wait_ge(stack_in[u][2], (unit // 2 + 1) * 16 * LOCAL_DMAS)
                for n in range(2):
                    bank = 2 * s + n
                    for k2 in range(2):
                        for half, keys in enumerate((ks, kb)):
                            for j in range(P // WIN):
                                c = (CT * s + 2 * n + k2) * P + j * WIN
                                first = WIN + c if half == 0 else c
                                col = (k2 * 2 + half) * P
                                ins = nc.tensor.matmul(ps[WIN * j:WIN * (j + 1), bank, col:col + P],
                                                       keys[u][:, first:first + WIN], qs[u][:, :, c:c + WIN],
                                                       start=True, stop=True)
                ins.then_inc(scored_l, 1)

            def local_weighted(step):
                unit, s = divmod(step, LOCAL_STEPS)
                pe.wait_ge(exped_l, step + 1)
                if step >= 2:
                    pe.wait_ge(acc_read_l, step - 1)
                if s == 0:
                    pe.wait_ge(v_ready_l, unit + 1)
                for t in range(CT):
                    for half in range(2):
                        ins = nc.tensor.matmul(ps[:, 4 + s, t * P:(t + 1) * P], v_diag[half][unit % 2][:, s * CT + t, :],
                                               probs_l[s][:, t // 2, ((t % 2) * 2 + half) * P:((t % 2) * 2 + half + 1) * P],
                                               start=half == 0, stop=half == 1)
                        if s == 1 and t == half == 0:
                            ins.then_inc(stack_free, 1)
                ins.then_inc(weighted_l, 1)

            pe.wait_ge(consts, 2)
            pe.wait_ge(read[7], value(PLANS["B"][-1].counts["use"], 1))
            for name in ("C", "D", "end"):
                steps = [item.step for item in PLANS[name] if item.kind == "local"]
                for item in PLANS[name]:
                    if item.kind == "local":
                        if item.step == steps[0]:
                            local_scores(item.step)
                        if item.step < steps[-1]:
                            local_scores(item.step + 1)
                        local_weighted(item.step)
                    else:
                        side(item)
    return nc


_INS = ["L0_attn_hidden", "L0_attn_norm1_w", "L0_attn_norm2_w", "L0_attn_g_wq", "L0_attn_g_kv_down",
        "L0_attn_g_k_up", "L0_attn_g_v_up", "L0_attn_g_wo", "L0_attn_l_wq", "L0_attn_l_wk", "L0_attn_l_wv",
        "L0_attn_l_wo", "L0_ffn_W1", "L0_ffn_b1", "L0_ffn_W2", "L0_ffn_b2"]


def rope_table():
    tab = np.zeros((SEQ, 2, 2 * HD), np.float32)
    for n, base in enumerate(BASES):
        inv = np.float32(1.0) / np.float32(base) ** (np.arange(0, HD, 2, dtype=np.float32) / np.float32(HD))
        angle = np.arange(SEQ, dtype=np.float32)[:, None] * inv[None, :].astype(np.float32)
        tab[:, n, 0:HD] = np.repeat(np.cos(angle), 2, axis=1)
        tab[:, n, HD:HD + HD // 2] = -np.sin(angle)
        tab[:, n, HD + HD // 2:] = np.sin(angle)
    return tab


def kernel(**inputs):
    import numpy as _np
    import concourse.bacc as _bacc
    from concourse import mybir as _mybir
    from concourse.bass_utils import run_bass_kernel_spmd as _run

    nc = _bacc.Bacc("TRN2", target_bir_lowering=False, num_devices=1)
    arrays, args = {}, []
    for name in _INS:
        a = _np.ascontiguousarray(inputs[name])
        arrays[f"in_{name}"] = a
        args.append(nc.dram_tensor(f"in_{name}", a.shape, _mybir.dt.from_np(a.dtype), kind="ExternalInput").ap())
    tab = rope_table()
    arrays["in_rope"] = tab
    args.append(nc.dram_tensor("in_rope", tab.shape, _mybir.dt.from_np(tab.dtype), kind="ExternalInput").ap())
    out = nc.dram_tensor("out_0", (BATCH, SEQ, D), _mybir.dt.float32, kind="ExternalOutput").ap()
    build(nc, *args, out)
    r = _run(nc, [arrays], core_ids=[0])
    return r.results[0]["out_0"]
```
